# Optimizing a Trainium2 kernel written in Bass

```python
import numpy as np
import jax
import jax.numpy as jnp

def _softmax(x, axis=-1):
    return jax.nn.softmax(x, axis=axis)

def _gelu(x):
    return jax.nn.gelu(x, approximate=True)

def _silu(x):
    return jax.nn.silu(x)

def _sigmoid(x):
    return jax.nn.sigmoid(x)

def _layernorm(x, axis=-1, eps=1e-05):
    m = jnp.mean(x, axis=axis, keepdims=True)
    v = jnp.var(x, axis=axis, keepdims=True)
    return (x - m) / jnp.sqrt(v + eps)

def _scatter_add(tgt, idx, src, axis=0):
    return tgt.at[idx].add(src)

def _segment_sum(src, seg, n):
    return jax.ops.segment_sum(src, seg, n)
kernel_name = 'mk_xattn_ffn_d1_seqx_r4_284fc3'

def setup_inputs(seed: int=0):
    np.random.seed(seed)
    _w = jnp.asarray

    def _rec_inputs():
        import jax
        import jax.numpy as jnp
        _rk = jax.random.key(seed)
        x = 0.002226 + 0.9996 * jax.random.normal(jax.random.fold_in(_rk, 1), (8, 256, 256), jnp.float32)
        _lenS = 256 - jax.random.randint(jax.random.fold_in(_rk, 7), (8,), 0, max(1, 256 // 4) + 1, jnp.int32)
        _lenS2 = 120 - jax.random.randint(jax.random.fold_in(_rk, 8), (8,), 0, max(1, 120 // 4) + 1, jnp.int32)
        _ctx_1024P = jax.random.normal(jax.random.fold_in(_rk, 11), (8, 16, 256), jnp.float32)
        _ctx_1024c = jax.random.dirichlet(jax.random.fold_in(_rk, 511), 0.3 * jnp.ones((16,), jnp.float32), (8, 120))
        _ctx_1024t = jnp.einsum('bsk,bkd->bsd', _ctx_1024c, _ctx_1024P)
        _ctx_1024t = _ctx_1024t * jax.lax.rsqrt(jnp.mean(jnp.square(_ctx_1024t)) + 1e-12) * 0.953939
        ctx_1024 = -0.000125008 + 0.999885 * (_ctx_1024t + 0.3 * jax.random.normal(jax.random.fold_in(_rk, 611), (8, 120, 256), jnp.float32))
        return (x, ctx_1024)
    x, ctx_1024 = _rec_inputs()

    def _L0_xattn_setup():
        import jax, jax.numpy as jnp
        import numpy as np
        EPS = 1e-05

        def layer_norm(x, g, b):
            mu = jnp.mean(x, axis=-1, keepdims=True)
            var = jnp.var(x, axis=-1, keepdims=True)
            return (x - mu) * jax.lax.rsqrt(var + EPS) * g + b
        key = jax.random.key(seed)
        ks = jax.random.split(key, 8)
        dim, heads, dim_head = (256, 16, 64)
        inner = heads * dim_head
        b, n, m = (8, 1024, 64)
        s = dim ** (-0.5)
        return {'x': jax.random.normal(ks[0], (b, n, dim), jnp.float32), 'latents': jax.random.normal(ks[1], (b, m, dim), jnp.float32), 'ln_m_g': jnp.ones((dim,), jnp.float32), 'ln_m_b': jnp.zeros((dim,), jnp.float32), 'ln_l_g': jnp.ones((dim,), jnp.float32), 'ln_l_b': jnp.zeros((dim,), jnp.float32), 'Wq': jax.random.normal(ks[2], (dim, inner), jnp.float32) * s, 'Wkv': jax.random.normal(ks[3], (dim, 2 * inner), jnp.float32) * s, 'Wout': jax.random.normal(ks[4], (inner, dim), jnp.float32) * s}
    _L0_xattn_all = _L0_xattn_setup()
    _L0_xattn_in = {k: v for k, v in _L0_xattn_all.items() if k in ('ln_m_g', 'ln_m_b', 'ln_l_g', 'ln_l_b', 'Wq', 'Wkv', 'Wout')}
    del _L0_xattn_all

    def _L0_ffn_setup():
        import jax, jax.numpy as jnp
        import numpy as np
        TOP_K = 2
        key = jax.random.key(seed)
        ks = jax.random.split(key, 5)
        B, T, D, F, E = (4, 512, 256, 1024, 8)
        s = 0.02
        return {'x': jax.random.normal(ks[0], (B, T, D), jnp.float32), 'gate_w': jax.random.normal(ks[1], (D, E), jnp.float32) * s, 'w1': jax.random.normal(ks[2], (E, D, F), jnp.float32) * s, 'w3': jax.random.normal(ks[3], (E, D, F), jnp.float32) * s, 'w2': jax.random.normal(ks[4], (E, F, D), jnp.float32) * s}
    _L0_ffn_all = _L0_ffn_setup()
    _L0_ffn_in = {k: v for k, v in _L0_ffn_all.items() if k in ('gate_w', 'w1', 'w3', 'w2')}
    del _L0_ffn_all
    return {'x': x, 'ctx_1024': ctx_1024, 'L0_xattn_ln_m_g': _L0_xattn_in['ln_m_g'], 'L0_xattn_ln_m_b': _L0_xattn_in['ln_m_b'], 'L0_xattn_ln_l_g': _L0_xattn_in['ln_l_g'], 'L0_xattn_ln_l_b': _L0_xattn_in['ln_l_b'], 'L0_xattn_Wq': _L0_xattn_in['Wq'], 'L0_xattn_Wkv': _L0_xattn_in['Wkv'], 'L0_xattn_Wout': _L0_xattn_in['Wout'], 'L0_ffn_gate_w': _L0_ffn_in['gate_w'], 'L0_ffn_w1': _L0_ffn_in['w1'], 'L0_ffn_w3': _L0_ffn_in['w3'], 'L0_ffn_w2': _L0_ffn_in['w2']}

def reference(x, ctx_1024, L0_xattn_ln_m_g, L0_xattn_ln_m_b, L0_xattn_ln_l_g, L0_xattn_ln_l_b, L0_xattn_Wq, L0_xattn_Wkv, L0_xattn_Wout, L0_ffn_gate_w, L0_ffn_w1, L0_ffn_w3, L0_ffn_w2):
    import jax
    import jax.numpy as jnp

    def _L0_xattn_ref(x, latents, ln_m_g, ln_m_b, ln_l_g, ln_l_b, Wq, Wkv, Wout):
        import jax, jax.numpy as jnp
        import numpy as np
        EPS = 1e-05

        def layer_norm(x, g, b):
            mu = jnp.mean(x, axis=-1, keepdims=True)
            var = jnp.var(x, axis=-1, keepdims=True)
            return (x - mu) * jax.lax.rsqrt(var + EPS) * g + b
        heads, dim_head = (16, 64)
        scale = dim_head ** (-0.5)
        x = layer_norm(x, ln_m_g, ln_m_b)
        lat = layer_norm(latents, ln_l_g, ln_l_b)
        b, m, _ = lat.shape
        q = lat @ Wq
        kv_input = jnp.concatenate([x, lat], axis=1)
        kv = kv_input @ Wkv
        k, v = jnp.split(kv, 2, axis=-1)

        def split_heads(t):
            return t.reshape(t.shape[0], t.shape[1], heads, dim_head).transpose(0, 2, 1, 3)
        q, k, v = (split_heads(q), split_heads(k), split_heads(v))
        dots = jnp.einsum('bhid,bhjd->bhij', q, k) * scale
        attn = jax.nn.softmax(dots, axis=-1)
        out = jnp.einsum('bhij,bhjd->bhid', attn, v)
        out = out.transpose(0, 2, 1, 3).reshape(b, m, heads * dim_head)
        return out @ Wout

    def _L0_ffn_ref(x, gate_w, w1, w3, w2):
        import jax, jax.numpy as jnp
        import numpy as np
        TOP_K = 2
        logits = jnp.einsum('btd,de->bte', x, gate_w)
        probs = jax.nn.softmax(logits, axis=-1)
        expert_weights, expert_indices = jax.lax.top_k(probs, TOP_K)
        expert_weights = expert_weights / expert_weights.sum(-1, keepdims=True)
        E = w1.shape[0]
        out = jnp.zeros_like(x)
        for i in range(E):
            wi = jnp.where(expert_indices == i, expert_weights, 0.0).sum(-1)
            h = jax.nn.silu(jnp.einsum('btd,df->btf', x, w1[i])) * jnp.einsum('btd,df->btf', x, w3[i])
            out = out + jnp.einsum('btf,fd->btd', h, w2[i]) * wi[..., None]
        return out
    x = x + _L0_xattn_ref(ctx_1024, _layernorm(x, axis=-1), L0_xattn_ln_m_g, L0_xattn_ln_m_b, L0_xattn_ln_l_g, L0_xattn_ln_l_b, L0_xattn_Wq, L0_xattn_Wkv, L0_xattn_Wout)
    x = x + _L0_ffn_ref(_layernorm(x, axis=-1), L0_ffn_gate_w, L0_ffn_w1, L0_ffn_w3, L0_ffn_w2)
    return x

_drawn_inputs = setup_inputs


def setup_inputs(seed=0):
    import zlib

    import numpy as np

    out = dict(_drawn_inputs(seed))
    spreads = {'L0_xattn_ln_m_g': (1.0, 0.2),
     'L0_xattn_ln_m_b': (0.0, 0.1),
     'L0_xattn_ln_l_g': (1.0, 0.2),
     'L0_xattn_ln_l_b': (0.0, 0.1)}
    factors = {'L0_ffn_gate_w': 8.467}
    for name, (base, spread) in spreads.items():
        noise = np.random.default_rng([zlib.crc32(name.encode()), seed]).standard_normal(out[name].shape)
        drawn = base * np.exp(spread * noise) if base else spread * noise
        out[name] = jnp.asarray(drawn.astype(out[name].dtype))
    for name, factor in factors.items():
        out[name] = (out[name] * factor).astype(out[name].dtype)
    return out
```

```python
import concourse.bass as bass
from concourse import mybir
from contextlib import ExitStack


def cross_attention_then_routed_ffn(
    nc: bass.Bass,
    x: bass.AP,
    context: bass.AP,
    ln_m_g: bass.AP,
    ln_m_b: bass.AP,
    ln_l_g: bass.AP,
    ln_l_b: bass.AP,
    Wq: bass.AP,
    Wkv: bass.AP,
    Wout: bass.AP,
    gate_w: bass.AP,
    w1: bass.AP,
    w3: bass.AP,
    w2: bass.AP,
    out: bass.AP,
):
    fp32, fp32r, bf16 = mybir.dt.float32, mybir.dt.float32r, mybir.dt.bfloat16
    i32, u32 = mybir.dt.int32, mybir.dt.uint32
    ALU = mybir.AluOpType
    ACT = mybir.ActivationFunctionType
    AX = mybir.AxisListType.X

    P = 128
    B, NQ, D = x.shape
    NCTX = context.shape[1]
    NKV = NCTX + NQ
    INNER = Wq.shape[1]
    DH = 64
    PAIRS = INNER // P
    DC = D // P
    QC = NQ // P
    KC = -(-NKV // P)
    KROWS = [min(P, NKV - P * c) for c in range(KC)]
    LNT = 1 + QC
    TPP = 2 * QC
    SCALE = DH ** -0.5
    HALF = INNER // 2
    EPS = 1e-5
    TOK = B * NQ // P
    E, _, F = w1.shape
    FC = F // P
    FH = F // 2
    TILES = (2 * B * NQ + E * P) // P
    SLOTS = TILES * P
    assert TILES % 2 == 0 and QC == 2 and DC == 2 and KC == 3 and PAIRS == 8
    PIECES = 6
    PW = DC * F // 2
    W3AT, W2AT, WCOLS = DC * F, 2 * DC * F, 2 * DC * F + FC * D

    x1_dram = nc.dram_tensor("x1_scratch", (TOK * P, D), fp32, kind="Internal").ap()
    xs_dram = nc.dram_tensor("slot_rows", (SLOTS, D), fp32, kind="Internal").ap()
    ys_dram = nc.dram_tensor("slot_outputs", (SLOTS, D), fp32, kind="Internal").ap()

    stack = ExitStack()
    sems = {}

    def sem(name):
        if name not in sems:
            sems[name] = stack.enter_context(nc.semaphore(name))
        return sems[name]

    with stack:
        def sb(name, shape, dt, ctx=stack):
            return ctx.enter_context(nc.sbuf_tensor(name, shape, dt))

        ident = sb("ident", [P, P], fp32)
        xn_all = sb("xn_all", [P, TOK, D], fp32)
        raw = sb("raw", [P, 2, PW], fp32)
        affine = sb("affine", [P, 4, DC], fp32)
        gate_sb = sb("gate_sb", [P, DC, E], fp32)
        w_top = sb("w_top", [P, 2, TOK], fp32)
        slot_of = sb("slot_of", [P, 2, TOK], u32)
        tile_parity = sb("tile_parity", [P, TILES], i32)
        tile_need = sb("tile_need", [P, TILES], i32)
        first_tile = sb("first_tile", [P, E], i32)

        attn = ExitStack()
        stage = sb("stage", [P, 4, 2048], fp32, attn)
        sb("stage_pad", [P, 4096], fp32, attn)
        wk_s = sb("wk_s", [P, 2, DC, INNER], fp32r, attn)
        wq_s = sb("wq_s", [P, 2, DC, INNER], fp32r, attn)
        wv_s = sb("wv_s", [P, 2, DC, INNER], fp32r, attn)
        wo_s = sb("wo_s", [P, 2, PAIRS, D], fp32r, attn)
        qT = sb("qT", [P, 2, 2, NQ], fp32r, attn)
        kT = sb("kT", [P, 2, 2, NKV], fp32r, attn)
        probs = sb("probs", [P, 2, TPP, KC * P], fp32, attn)
        probsT = sb("probsT", [P, TPP, KC, P], fp32, attn)
        v_sb = sb("v_sb", [P, KC, INNER], fp32, attn)
        kvT_f = sb("kvT_f", [P, DC, NKV], fp32, attn)
        kvT = sb("kvT", [P, 2, DC, NKV], fp32r, attn)
        xin = sb("xin", [P, LNT, D], fp32, attn)
        z = sb("z", [P, LNT, D], fp32, attn)
        xres = sb("xres", [P, QC, D], fp32, attn)
        x1 = sb("x1", [P, QC, D], fp32, attn)
        o_sb = sb("o_sb", [P, QC, P], fp32, attn)
        oT = sb("oT", [P, 2, QC * P], fp32r, attn)
        negmax = sb("negmax", [P, 2, TPP], fp32, attn)
        rowsum = sb("rowsum", [P, 2, TPP], fp32, attn)
        rinv = sb("rinv", [P, TPP], fp32, attn)
        stats = sb("stats", [P, LNT, 6], fp32, attn)
        mv = sb("mv", [P, LNT, 2], fp32, attn)
        nve = sb("nve", [P, LNT], fp32, attn)
        nt = sb("nt", [P, LNT], fp32, attn)
        rstd = sb("rstd", [P, LNT], fp32, attn)
        attn.close()

        W = sb("W", [P, 2, 2, WCOLS], fp32r)
        zero = sb("zero", [P, D], fp32)
        xnT = sb("xnT", [P, 2, DC, P], fp32)
        lg = sb("lg", [P, TOK, E], fp32)
        mx = sb("mx", [P, TOK], fp32)
        ex = sb("ex", [P, TOK, E], fp32)
        top = sb("top", [P, TOK, 8], fp32)
        topi = sb("topi", [P, TOK, 8], u32)
        topf = sb("topf", [P, TOK, 8], fp32)
        pick = sb("pick", [P, 2, TOK, E], fp32)
        both = sb("both", [P, TOK, E], bf16)
        tri = sb("tri", [P, P], bf16)
        ones = sb("ones", [P, P], bf16)
        iota_i = sb("iota_i", [P, TILES], i32)
        iota_f = sb("iota_f", [P, TILES], fp32)
        count = sb("count", [P, E], fp32)
        wide = sb("wide", [P, TILES * E], fp32)
        before = sb("before", [P, E, E], fp32)
        tiles_of = sb("tiles_of", [P, E], fp32)
        first_f = sb("first_f", [P, E], fp32)
        base_f = sb("base_f", [P, E], fp32)
        slot_f = sb("slot_f", [P, TOK, E], fp32)
        slot_k = sb("slot_k", [P, 2, TOK], fp32)
        need_f = sb("need_f", [P, TILES], fp32)
        xg = sb("xg", [P, 2, D], fp32)
        xgT = sb("xgT", [P, 2, 2, DC, P], fp32r)
        act_h = sb("act_h", [P, 2, FH], fp32)
        g_sb = sb("g_sb", [P, 2, FH], fp32)
        gT = sb("gT", [P, 2, FC, P], fp32r)
        y_sb = sb("y_sb", [P, 2, D], fp32)
        yk = sb("yk", [P, 4, 2, D], fp32)
        xf = sb("xf", [P, 4, D], fp32)

        banks = [stack.enter_context(nc.psum_tensor(f"bank{n}", [P, 512], fp32)) for n in range(8)]
        PROJ, SCORE, TRANS, ACC, HEADS = banks[0:2], banks[2:4], banks[4:6], banks[6], banks[7]

        def wait(eng, s, value):
            if not (isinstance(value, int) and value <= 0):
                eng.wait_ge(s, value)

        def split_product(outp, stationary, moving, first, last, **kw):
            for n, (a, b) in enumerate(((0, 0), (0, 1), (1, 0))):
                ins = nc.tensor.matmul(outp, stationary(a), moving(b), start=first and n == 0,
                                       stop=last and n == 2, **kw)
            return ins

        ITEMS = [["q", "k"] for _ in range(PAIRS)]
        ITEMS[1] += [("v", 1, c) for c in range(KC)]
        ITEMS[6] += [("x", 0, d) for d in range(DC)]
        ITEMS[7] += [("v", 0, c) for c in range(KC)]
        OFFSET = [sum(len(i) for i in ITEMS[:q]) for q in range(PAIRS + 1)]
        AHEAD = DC + 2 + KC
        assert OFFSET[PAIRS] % 2 == 0

        def step_items(b, q):
            b, q = b + q // PAIRS, q % PAIRS
            found = []
            for n, what in enumerate(ITEMS[q]):
                ahead = what[0] == "x" or what[:2] == ("v", 0) or (q == PAIRS - 1 and what in ("q", "k"))
                if not (isinstance(b, int) and b + ahead >= B):
                    found.append((b * OFFSET[PAIRS] + (AHEAD + OFFSET[q] + n), (AHEAD + OFFSET[q] + n) % 2,
                                  what, b + 1 if ahead else b))
            return found

        FIRST_X = [(d, d % 2, ("x", 0, d), 0) for d in range(DC)]
        FIRST_QKV = [(DC + n, (DC + n) % 2, what, 0) for n, what in enumerate(["q", "k"] + [("v", 0, c) for c in range(KC)])]

        def steps(eng, step):
            step(0, 0)
            step(0, 1)
            with eng.Fori(0, B - 1) as b:
                for q in range(2, PAIRS + 2):
                    step(b, q)
            for q in range(2, PAIRS + 2):
                step(B - 1, q)

        def stage_on(b, q, lag):
            return not (isinstance(b, int) and not 0 <= b * PAIRS + q - lag < B * PAIRS)

        def tile_steps(eng, step):
            for t in range(3):
                step(t, t % 2, t // 2)
            with eng.Fori(1, TILES // 2 - 1) as i:
                step(2 * i + 1, 1, i)
                step(2 * i + 2, 0, i + 1)
            step(TILES - 1, 1, TILES // 2 - 1)
            step(TILES, 0, TILES // 2)

        def tile_on(t):
            return not (isinstance(t, int) and not 0 <= t < TILES)

        xin_loaded, xin_free = sem("xin_loaded"), sem("xin_free")
        xres_loaded, x1_stored = sem("xres_loaded"), sem("x1_stored")
        small_loaded, stage_loaded = sem("small_loaded"), sem("stage_loaded")
        w_hi, w_ready = sem("w_hi"), sem("w_ready")
        consts, turns_taken = sem("consts"), sem("turns_taken")
        prep_step, fin_step, route_step = sem("prep_step"), sem("fin_step"), sem("route_step")
        z_ready, affine_done, kvT_ready = sem("z_ready"), sem("affine_done"), sem("kvT_ready")
        proj_done, proj_free = sem("proj_done"), sem("proj_free")
        qk_hi, qk_ready, v_ready = sem("qk_hi"), sem("qk_ready"), sem("v_ready")
        scores_done, max_done, exp_done = sem("scores_done"), sem("max_done"), sem("exp_done")
        trans_done, pt_act, pt_dve, av_done = sem("trans_done"), sem("pt_act"), sem("pt_dve"), sem("av_done")
        rinv_done, o_ready = sem("rinv_done"), sem("o_ready")
        oT_done, oT_hi, oT_ready, wout_done = sem("oT_done"), sem("oT_hi"), sem("oT_ready"), sem("wout_done")
        x1_ready, xn_ready = sem("x1_ready"), sem("xn_ready")
        raw_loaded, raw_hi, pieces_ready = [sem(f"raw_loaded{n}") for n in range(2)], sem("raw_hi"), sem("pieces_ready")
        zero_set, xs_zeroed, scattered = sem("zero_set"), sem("xs_zeroed"), sem("scattered")
        xnT_done, xnT_ready, gates_done, lg_done = sem("xnT_done"), sem("xnT_ready"), sem("gates_done"), sem("lg_done")
        gate_exp, routed, both_ready, ranks_done = sem("gate_exp"), sem("routed"), sem("both_ready"), sem("ranks_done")
        xg_loaded, xg_trans, xg_hi, xg_ready = [sem(f"xg_loaded{n}") for n in range(2)], sem("xg_trans"), sem("xg_hi"), sem("xg_ready")
        h_done, silu_done, g_done = sem("h_done"), sem("silu_done"), sem("g_done")
        gT_done, gT_hi, gT_ready = sem("gT_done"), sem("gT_hi"), sem("gT_ready")
        y_done, y_copied, y_stored = sem("y_done"), sem("y_copied"), [sem(f"y_stored{n}") for n in range(2)]
        yk_gathered, xf_loaded, half_sum, out_ready, out_stored = (
            [sem(f"yk_gathered{n}") for n in range(4)], [sem(f"xf_loaded{n}") for n in range(4)], sem("half_sum"),
            sem("out_ready"), [sem(f"out_stored{n}") for n in range(4)])

        block = stack.enter_context(nc.Block())

        x_rows = x.rearrange("b (c p) d -> b p c d", p=P)
        x1_rows = x1_dram.rearrange("(b c p) d -> b p c d", p=P, c=QC)
        xs_rows = xs_dram.rearrange("(t p) d -> t p d", p=P)
        ys_rows = ys_dram.rearrange("(t p) d -> t p d", p=P)
        out_rows = out.rearrange("b (c p) d -> (b c) p d", p=P)
        x1_tiles = x1_dram.rearrange("(t p) d -> t p d", p=P)

        def zero_fill_source():
            return zero[:, :].rearrange("p (o d) -> p o d", o=1).broadcast_to([P, TILES, D])

        @block.sync
        def _(sp):
            def load_xin(b):
                wait(sp, xin_free, b)
                sp.dma_start(xin[0:NCTX, 0, :], context[b]).then_inc(xin_loaded, 16)
                sp.dma_start(xin[:, 1:LNT, :], x_rows[b]).then_inc(xin_loaded, 16)

            def load_xres(b):
                if not isinstance(b, int):
                    sp.wait_ge(x1_stored, 16 * b)
                sp.dma_start(xres[:, :, :], x_rows[b]).then_inc(xres_loaded, 16)

            def store_x1(b):
                sp.wait_ge(x1_ready, 1 + b + 1)
                sp.dma_start(x1_rows[b], x1[:, :, :]).then_inc(x1_stored, 16)

            sp.wait_ge(consts, 1)
            load_xin(0)
            sp.dma_start(stage[:, 0, :].rearrange("p (c n) -> p c n", c=DC),
                         Wkv[:, 0:INNER].rearrange("(c p) n -> p c n", p=P)).then_inc(stage_loaded, 16)
            sp.dma_start(stage[:, 1, :].rearrange("p (c n) -> p c n", c=DC),
                         Wq.rearrange("(c p) n -> p c n", p=P)).then_inc(stage_loaded, 16)
            sp.dma_start(stage[:, 2, :].rearrange("p (c n) -> p c n", c=DC),
                         Wkv[:, INNER:2 * INNER].rearrange("(c p) n -> p c n", p=P)).then_inc(stage_loaded, 16)
            sp.dma_start(stage[:, 3, :].rearrange("p (c n) -> p c n", c=PAIRS),
                         Wout.rearrange("(c p) n -> p c n", p=P)).then_inc(stage_loaded, 16)
            for n, vector in enumerate((ln_m_g, ln_m_b, ln_l_g, ln_l_b)):
                sp.dma_start(affine[:, n, :], vector.rearrange("(c p) -> p c", p=P), allow_slow_non_contiguous=True).then_inc(small_loaded, 16)
            sp.dma_start(gate_sb[:, :, :], gate_w.rearrange("(c p) e -> p c e", p=P)).then_inc(small_loaded, 16)
            load_xres(0)
            with sp.Fori(0, B - 1) as b:
                load_xin(b + 1)
                store_x1(b)
                load_xres(b + 1)
            store_x1(B - 1)

            sp.wait_ge(zero_set, 1)
            sp.dma_start(xs_dram.rearrange("(t p) d -> p t d", p=P), zero_fill_source()).then_inc(xs_zeroed, 16)

            def load_slots(t, par):
                if tile_on(t):
                    wait(sp, xg_trans, t - 1)
                    sp.dma_start(xg[:, par, :], xs_rows[t]).then_inc(xg_loaded[par], 16)

            def store_y(t, par):
                sp.wait_ge(y_copied, t + 1)
                sp.dma_start(ys_rows[t], y_sb[:, par, :]).then_inc(y_stored[par], 16)

            sp.wait_ge(scattered, 32 * TOK)
            load_slots(0, 0)
            load_slots(1, 1)

            def step(t, par):
                load_slots(t + 2 if not isinstance(t, int) or t + 2 < TILES else TILES, par)
                if not isinstance(t, int) or t >= 1:
                    store_y(t - 1, 1 - par)

            step(0, 0)
            with sp.Fori(0, TILES // 2 - 2) as i:
                step(2 * i + 1, 1)
                step(2 * i + 2, 0)
            for t in range(TILES - 3, TILES + 1):
                step(t, t % 2)

            for i in range(TOK):
                wait(sp, out_ready, i - 3)
                wait(sp, out_stored[i % 4], 16 * (i // 4))
                sp.dma_start(xf[:, i % 4, :], x1_tiles[i]).then_inc(xf_loaded[i % 4], 16)
                if i >= 2:
                    sp.wait_ge(out_ready, i - 1)
                    sp.dma_start(out_rows[i - 2], xf[:, (i - 2) % 4, :]).then_inc(out_stored[(i - 2) % 4], 16)
            for i in (TOK - 2, TOK - 1):
                sp.wait_ge(out_ready, i + 1)
                sp.dma_start(out_rows[i], xf[:, i % 4, :]).then_inc(out_stored[i % 4], 16)
            for s in out_stored:
                sp.wait_ge(s, 16 * TOK // 4)
            sp.wait_ge(x1_stored, 16 * B)

        @block.gpsimd
        def _(pool):
            nc.gpsimd.memset(xin[:, 0, :], 0.0).then_inc(consts, 1)
            nc.gpsimd.memset(ident[:, :], 0.0).then_inc(consts, 1)
            pool.wait_ge(consts, 2)
            nc.gpsimd.affine_select(out=ident[:, :], in_=ident[:, :], compare_op=ALU.not_equal, fill=1.0,
                                    base=0, pattern=[[-1, P]], channel_multiplier=1).then_inc(consts, 1)
            nc.gpsimd.memset(probs[:, :, :, NKV:KC * P], 0.0).then_inc(consts, 1)

            def load_piece(e, n):
                if n < 2 * DC:
                    src = (w1, w3)[n // DC][e, (n % DC) * P:(n % DC + 1) * P, :]
                    dst = raw[:, n % 2, :]
                else:
                    src = w2[e, (n - 2 * DC) * FH:(n - 2 * DC + 1) * FH, :].rearrange("(c p) d -> p c d", p=P)
                    dst = raw[:, n % 2, :].rearrange("p (c d) -> p c d", d=D)
                pool.dma_start(dst, src).then_inc(raw_loaded[n % 2], 16)

            def split_expert(e):
                for n in range(PIECES):
                    k = e * PIECES + n
                    cols = slice(n * PW, (n + 1) * PW)
                    pool.wait_ge(raw_loaded[n % 2], 16 * (k // 2 + 1))
                    nc.gpsimd.tensor_copy(W[:, e % 2, 0, cols], raw[:, n % 2, :]).then_inc(raw_hi, 1)
                    pool.wait_ge(raw_hi, k + 1)
                    nc.gpsimd.tensor_tensor(W[:, e % 2, 1, cols], raw[:, n % 2, :], W[:, e % 2, 0, cols],
                                            ALU.subtract).then_inc(pieces_ready, 1)
                    if k + 2 < E * PIECES:
                        pool.wait_ge(pieces_ready, k + 1)
                        load_piece((k + 2) // PIECES, (k + 2) % PIECES)

            load_piece(0, 0)
            load_piece(0, 1)

            def split_kvT(b):
                for d in range(DC):
                    pool.wait_ge(affine_done, 2 * DC * b + 2 * (d + 1))
                    pool.sem_inc(turns_taken, 1)
                    nc.gpsimd.tensor_copy(kvT[:, 0, d, :], kvT_f[:, d, :]).then_inc(kvT_ready, 1)
                    pool.wait_ge(kvT_ready, 2 * DC * b + 2 * d + 1)
                    nc.gpsimd.tensor_tensor(kvT[:, 1, d, :], kvT_f[:, d, :], kvT[:, 0, d, :],
                                            ALU.subtract).then_inc(kvT_ready, 1)

            split_kvT(0)
            pool.wait_ge(w_ready, 4)
            split_expert(0)
            with pool.Fori(1, B) as b:
                split_kvT(b)

            pool.wait_ge(xn_ready, TOK)
            nc.gpsimd.memset(zero[:, :], 0.0).then_inc(zero_set, 1)
            nc.gpsimd.iota(iota_i[:, :], pattern=[[1, TILES]], base=0, channel_multiplier=0).then_inc(consts, 1)
            nc.gpsimd.memset(ones[:, :], 1.0).then_inc(consts, 1)
            nc.gpsimd.memset(before[:, :, :], 1.0).then_inc(consts, 1)
            pool.wait_ge(consts, 7)
            nc.gpsimd.affine_select(out=tri[:, :], in_=ones[:, :], compare_op=ALU.is_gt, fill=0.0, base=0,
                                    pattern=[[1, P]], channel_multiplier=-1).then_inc(consts, 1)
            nc.gpsimd.affine_select(out=before[:, :, :], in_=before[:, :, :], compare_op=ALU.is_gt, fill=0.0,
                                    base=0, pattern=[[1, E], [-1, E]], channel_multiplier=0).then_inc(consts, 1)

            pool.wait_ge(xs_zeroed, 16)
            pool.wait_ge(routed, 1)
            for i in range(TOK):
                for k in range(2):
                    nc.gpsimd.indirect_dma_start(
                        out=xs_dram, out_offset=bass.IndirectOffsetOnAxis(ap=slot_of[:, k, i:i + 1], axis=0),
                        in_=xn_all[:, i, :], in_offset=None).then_inc(scattered, 16)
            for e in range(1, E):
                if e >= 2:
                    start = pool.value_load(first_tile[0:1, e - 1:e], min_val=0, max_val=TILES)
                    pool.wait_ge(y_done, start)
                    pool.sem_inc(turns_taken, 1)
                split_expert(e)

            for s in y_stored:
                pool.wait_ge(s, 16 * TILES // 2)
            for i in range(TOK):
                wait(pool, out_ready, i - 3)
                for k in range(2):
                    nc.gpsimd.indirect_dma_start(
                        out=yk[:, i % 4, k, :], out_offset=None, in_=ys_dram,
                        in_offset=bass.IndirectOffsetOnAxis(ap=slot_of[:, k, i:i + 1], axis=0)).then_inc(yk_gathered[i % 4], 16)

        @block.scalar
        def _(act):
            def q_or_k_hi(n, bank, what, x_pair, par):
                act.wait_ge(proj_done, n + 1)
                if what == "q":
                    nc.scalar.activation(qT[:, par, 0, :], PROJ[bank][:, 0:NQ], ACT.Copy, scale=SCALE).then_inc(qk_hi, 1)
                else:
                    nc.scalar.activation(kT[:, par, 0, :], PROJ[bank][:, 0:NKV], ACT.Copy).then_inc(qk_hi, 1)

            for n, w in enumerate((wk_s, wq_s, wv_s, wo_s)):
                act.wait_ge(stage_loaded, 16 * 4)
                nc.scalar.activation(w[:, 0, :, :], stage[:, n, :].rearrange("p (c m) -> p c m", c=w.shape[2]),
                                     ACT.Copy).then_inc(w_hi, 1)
            for item in FIRST_QKV[0:2]:
                q_or_k_hi(*item[:3], 0, 0)
            act.wait_ge(consts, 4)

            def step(b, q):
                s = b * PAIRS + q
                if stage_on(b, q, 2):
                    act.wait_ge(oT_done, s - 1)
                    act.wait_ge(wout_done, 1 + s - 2)
                    nc.scalar.activation(oT[:, 0, :], HEADS[:, QC * P:2 * QC * P], ACT.Copy).then_inc(oT_hi, 1)
                if stage_on(b, q, -1):
                    wait(act, scores_done, TPP * s)
                    for item in step_items(b, q)[0:2]:
                        q_or_k_hi(*item[:3], s, (q + 1) % 2)
                for j in range(TPP):
                    if stage_on(b, q, 0):
                        t = s * TPP + j
                        act.wait_ge(max_done, t + 1)
                        wait(act, trans_done, t - 7)
                        nc.scalar.activation(probs[:, q % 2, j, 0:NKV], SCORE[j % 2][:, 0:NKV], ACT.Exp,
                                             bias=negmax[:, q % 2, j:j + 1],
                                             accum_out=rowsum[:, q % 2, j:j + 1]).then_inc(exp_done, 1)
                    if stage_on(b, q, 1) and j % 2 == 0:
                        t = (s - 1) * TPP + j
                        act.wait_ge(trans_done, t + 1)
                        wait(act, av_done, t - 3)
                        nc.scalar.activation(probsT[:, j, :, :], TRANS[0][:, 0:KC * P].rearrange("p (c n) -> p c n", c=KC),
                                             ACT.Copy).then_inc(pt_act, 1)

            steps(act, step)

            act.wait_ge(lg_done, 1)
            nc.scalar.activation(ex[:, :, :], lg[:, :, :], ACT.Exp).then_inc(gate_exp, 1)

            def xg_split(t, par):
                act.wait_ge(xg_trans, t + 1)
                wait(act, h_done, 4 * (t - 1))
                nc.scalar.activation(xgT[:, par, 0, :, :], HEADS[:, 0:D].rearrange("p (c n) -> p c n", c=DC),
                                     ACT.Copy).then_inc(xg_hi, 1)

            xg_split(0, 0)

            def tile_step(t, par, u):
                if tile_on(t + 1):
                    xg_split(t + 1, 1 - par)
                if tile_on(t - 1):
                    for half in range(2):
                        act.wait_ge(gT_done, 2 * (t - 1) + half + 1)
                        wait(act, y_done, t - 1)
                        nc.scalar.activation(gT[:, 0, 4 * half:4 * half + 4, :],
                                             banks[4 + half][:, :].rearrange("p (c n) -> p c n", c=4),
                                             ACT.Copy).then_inc(gT_hi, 1)
                if tile_on(t):
                    for half in range(2):
                        act.wait_ge(h_done, 4 * t + 2 * half + 1)
                        wait(act, g_done, 2 * (t - 1) + half + 1)
                        nc.scalar.activation(act_h[:, half, :], banks[2 * half][:, :], ACT.Silu).then_inc(silu_done, 1)

            tile_steps(act, tile_step)

        @block.vector
        def _(dve):
            def chain(s, start):
                at = [0]

                def link(ins):
                    at[0] += 1
                    ins.then_inc(s, 1)
                    dve.wait_ge(s, start + at[0])
                return link, at

            def rsqrt(link, n):
                y, ve, t = rstd[:, 0:n], nve[:, 0:n], nt[:, 0:n]
                link(nc.vector.tensor_scalar(ve, mv[:, 0:n, 1], EPS, None, ALU.add))
                link(nc.vector.tensor_scalar(t.bitcast(i32), ve.bitcast(i32), 1, None, ALU.logical_shift_right))
                link(nc.vector.tensor_scalar(y.bitcast(i32), t.bitcast(i32), -1.0, float(0x5F3759DF), ALU.mult, ALU.add))
                for _ in range(3):
                    link(nc.vector.scalar_tensor_tensor(t, y, -0.5, y, ALU.mult, ALU.mult))
                    link(nc.vector.tensor_tensor(t, t, ve, ALU.mult))
                    link(nc.vector.scalar_tensor_tensor(y, t, 1.5, y, ALU.add, ALU.mult))

            def moments(link, tiles):
                for n, tile in enumerate(tiles):
                    ins = nc.vector.bn_stats(stats[:, n, :], tile)
                link(ins)
                dve.sem_inc(turns_taken, 1)
                for n in range(len(tiles)):
                    ins = nc.vector.bn_aggr(mv[:, n, :], stats[:, n, :])
                link(ins)

            def normalise(outp, inp, n):
                return nc.vector.tensor_scalar(outp, inp, mv[:, n, 0:1], rstd[:, n:n + 1], ALU.subtract, ALU.mult)

            RSQRT, PREP, FIN = 12, 2 * (2 + 12) + 1, 2 + 12

            def prepare(b):
                link, at = chain(prep_step, b * PREP)
                dve.wait_ge(xin_loaded, 32 * (b + 1))
                moments(link, [xin[:, n, :] for n in range(LNT)])
                rsqrt(link, LNT)
                for n in range(LNT):
                    ins = normalise(z[:, n, :], xin[:, n, :], n)
                ins.then_inc(xin_free, 1)
                dve.wait_ge(xin_free, b + 1)
                moments(link, [z[:, n, :] for n in range(1, LNT)])
                rsqrt(link, QC)
                for n in range(QC):
                    ins = normalise(z[:, 1 + n, :], z[:, 1 + n, :], n)
                    if n == 0:
                        link(ins)
                ins.then_inc(z_ready, 1)
                assert at[0] == PREP

            def finish_batch(b):
                dve.wait_ge(wout_done, 1 + PAIRS * (b + 1))
                dve.wait_ge(xres_loaded, 16 * (b + 1))
                nc.vector.tensor_tensor(x1[:, :, :], ACC[:, :].rearrange("p (c d) -> p c d", c=QC), xres[:, :, :],
                                        ALU.add).then_inc(x1_ready, 1)
                dve.wait_ge(x1_ready, 1 + b + 1)
                link, at = chain(fin_step, b * FIN)
                moments(link, [x1[:, n, :] for n in range(QC)])
                rsqrt(link, QC)
                for n in range(QC):
                    normalise(xn_all[:, b * QC + n, :], x1[:, n, :], n).then_inc(xn_ready, 1)
                assert at[0] == FIN

            def evacuate(n, bank, what, b, pair, par):
                src = PROJ[bank]
                if what == "q":
                    dve.wait_ge(qk_hi, 2 * pair + 1)
                    nc.vector.scalar_tensor_tensor(qT[:, par, 1, :], src[:, 0:NQ], SCALE, qT[:, par, 0, :],
                                                   ALU.mult, ALU.subtract).then_inc(qk_ready, 1)
                    dve.wait_ge(qk_ready, 2 * pair + 1)
                elif what == "k":
                    dve.wait_ge(qk_hi, 2 * pair + 2)
                    nc.vector.tensor_tensor(kT[:, par, 1, :], src[:, 0:NKV], kT[:, par, 0, :],
                                            ALU.subtract).then_inc(qk_ready, 1)
                    dve.wait_ge(qk_ready, 2 * pair + 2)
                elif what[0] == "x":
                    d = what[2]
                    dve.wait_ge(proj_done, n + 1)
                    wait(dve, kvT_ready, 2 * DC * b)
                    for lo, hi, g in ((0, NCTX, 0), (NCTX, NKV, 2)):
                        nc.vector.tensor_scalar(kvT_f[:, d, lo:hi], src[:, lo:hi], affine[:, g, d:d + 1],
                                                affine[:, g + 1, d:d + 1], ALU.mult, ALU.add).then_inc(affine_done, 1)
                    dve.wait_ge(affine_done, 2 * DC * b + 2 * (d + 1))
                else:
                    half, c = what[1], what[2]
                    dve.wait_ge(proj_done, n + 1)
                    nc.vector.tensor_copy(v_sb[0:KROWS[c], c, half * HALF:(half + 1) * HALF],
                                          src[0:KROWS[c], :]).then_inc(v_ready, 1)
                    dve.wait_ge(v_ready, 2 * KC * b + KC * half + c + 1)
                nc.vector.sem_inc(proj_free, 1)

            dve.sem_inc(x1_ready, 1)
            prepare(0)
            dve.wait_ge(small_loaded, 16 * 5)
            for item in FIRST_X:
                evacuate(*item, 0, 0)
            for n, w in enumerate((wk_s, wq_s, wv_s, wo_s)):
                dve.wait_ge(w_hi, n + 1)
                nc.vector.tensor_tensor(w[:, 1, :, :], stage[:, n, :].rearrange("p (c m) -> p c m", c=w.shape[2]),
                                        w[:, 0, :, :], ALU.subtract).then_inc(w_ready, 1)
            for item in FIRST_QKV:
                evacuate(*item, 0, 0)

            def heads_out(s, par):
                dve.wait_ge(exp_done, TPP * (s + 1))
                wait(dve, o_ready, s)
                nc.vector.reciprocal(rinv[:, :], rowsum[:, par, :]).then_inc(rinv_done, 1)
                dve.wait_ge(rinv_done, s + 1)
                dve.wait_ge(av_done, TPP * (s + 1))
                wait(dve, oT_done, s)
                nc.vector.tensor_tensor(o_sb[:, :, :].rearrange("p c (h d) -> p (c h) d", h=2),
                                        HEADS[:, 0:QC * P].rearrange("p (j d) -> p j d", d=DH),
                                        rinv[:, :].rearrange("p (j o) -> p j o", o=1).broadcast_to([P, TPP, DH]),
                                        ALU.mult).then_inc(o_ready, 1)

            def step(b, q):
                s = b * PAIRS + q
                items = step_items(b, q)
                if stage_on(b, q, 2):
                    dve.wait_ge(oT_hi, s - 1)
                    nc.vector.tensor_tensor(oT[:, 1, :], HEADS[:, QC * P:2 * QC * P], oT[:, 0, :],
                                            ALU.subtract).then_inc(oT_ready, 1)
                for item in items:
                    if item[2] in ("q", "k"):
                        evacuate(*item, s + 1, (q + 1) % 2)
                for j in range(TPP):
                    if stage_on(b, q, 0):
                        dve.wait_ge(scores_done, s * TPP + j + 1)
                        nc.vector.tensor_reduce(negmax[:, q % 2, j:j + 1], SCORE[j % 2][:, 0:NKV], AX, ALU.max,
                                                negate=True).then_inc(max_done, 1)
                    if stage_on(b, q, 1) and j % 2 == 1:
                        t = (s - 1) * TPP + j
                        dve.wait_ge(trans_done, t + 1)
                        wait(dve, av_done, t - 3)
                        nc.vector.tensor_copy(probsT[:, j, :, :], TRANS[1][:, 0:KC * P].rearrange("p (c n) -> p c n", c=KC)
                                              ).then_inc(pt_dve, 1)
                if stage_on(b, q, 1):
                    heads_out(s - 1, (q + 1) % 2)
                for item in items:
                    if item[2] not in ("q", "k"):
                        evacuate(*item, 0, 0)
                if q == 3 and not (isinstance(b, int) and b == B - 1):
                    prepare(b + 1)
                if q == PAIRS + 1:
                    finish_batch(b)

            steps(dve, step)

            dve.wait_ge(xn_ready, TOK)
            for i in range(TOK):
                dve.wait_ge(xnT_done, i + 1)
                wait(dve, gates_done, i - 1)
                nc.vector.tensor_copy(xnT[:, i % 2, :, :], PROJ[i % 2][:, 0:D].rearrange("p (c n) -> p c n", c=DC)
                                      ).then_inc(xnT_ready, 1)
            link, _ = chain(route_step, 0)
            dve.wait_ge(gates_done, TOK)
            dve.wait_ge(consts, 9)
            v = nc.vector

            def wide_as(shape):
                n = 1
                for m in shape[1:]:
                    n *= m
                names = "abc"[:len(shape) - 1]
                sizes = dict(zip(names, shape[1:]))
                return wide[:, 0:n].rearrange(f"p ({' '.join(names)}) -> p {' '.join(names)}", **sizes)

            def spread(ap, shape, at):
                return ap.unsqueeze(at).broadcast_to(shape)

            TE = [P, TOK, E]
            gates = SCORE[0][:, 0:TOK * E].rearrange("p (i e) -> p i e", e=E)
            link(v.tensor_reduce(mx[:, :], gates, AX, ALU.max))
            v.tensor_tensor(lg[:, :, :], gates, spread(mx[:, :], TE, 2), ALU.subtract).then_inc(lg_done, 1)
            dve.wait_ge(gate_exp, 1)
            link(v.tensor_reduce(mx[:, :], ex[:, :, :], AX, ALU.add))
            link(v.reciprocal(mx[:, :], mx[:, :]))
            link(v.tensor_tensor(ex[:, :, :], ex[:, :, :], spread(mx[:, :], TE, 2), ALU.mult))
            for i in range(TOK):
                ins = v.max(top[:, i, :], ex[:, i, :])
            link(ins)
            for i in range(TOK):
                ins = v.max_index(topi[:, i, :], top[:, i, :], ex[:, i, :])
            link(ins)
            link(v.tensor_copy(topf[:, :, 0:2], topi[:, :, 0:2]))
            link(v.tensor_copy(iota_f[:, :], iota_i[:, :]))
            for k in range(2):
                link(v.tensor_tensor(pick[:, k, :, :], spread(topf[:, :, k], TE, 2),
                                     spread(iota_f[:, 0:E], TE, 1), ALU.is_equal))
            v.tensor_tensor(both[:, :, :], pick[:, 0, :, :], pick[:, 1, :, :], ALU.add).then_inc(both_ready, 1)
            link(v.tensor_tensor(mx[:, :], top[:, :, 0], top[:, :, 1], ALU.add))
            link(v.reciprocal(mx[:, :], mx[:, :]))
            link(v.tensor_tensor(w_top[:, :, :], top[:, :, 0:2].rearrange("p i k -> p k i"),
                                 spread(mx[:, :], [P, 2, TOK], 1), ALU.mult))
            dve.wait_ge(ranks_done, 2)
            link(v.tensor_copy(count[:, :], SCORE[1][:, TOK * E:TOK * E + E]))
            steps_of = TOK - 1
            link(v.tensor_scalar(need_f[:, 0:steps_of], iota_f[:, 1:TOK], float(P), None, ALU.mult))
            shape = [P, E, steps_of]
            link(v.tensor_tensor(wide_as(shape), spread(count[:, :], shape, 2),
                                 spread(need_f[:, 0:steps_of], shape, 1), ALU.is_gt))
            link(v.tensor_reduce(tiles_of[:, :], wide_as(shape), AX, ALU.add))
            link(v.tensor_scalar(tiles_of[:, :], tiles_of[:, :], 1.0, None, ALU.add))
            shape = [P, E, E]
            link(v.tensor_tensor(wide_as(shape), before[:, :, :], spread(tiles_of[:, :], shape, 1), ALU.mult))
            link(v.tensor_reduce(first_f[:, :], wide_as(shape), AX, ALU.add))
            link(v.tensor_copy(first_tile[:, :], first_f[:, :]))
            link(v.tensor_scalar(base_f[:, :], first_f[:, :], float(P), None, ALU.mult))
            link(v.tensor_tensor(slot_f[:, :, :], SCORE[1][:, 0:TOK * E].rearrange("p (i e) -> p i e", e=E),
                                 spread(base_f[:, :], TE, 1), ALU.add))
            for k in range(2):
                link(v.tensor_tensor(wide_as(TE), pick[:, k, :, :], slot_f[:, :, :], ALU.mult))
                link(v.tensor_reduce(slot_k[:, k, :], wide_as(TE), AX, ALU.add))
            link(v.tensor_copy(slot_of[:, :, :], slot_k[:, :, :]))
            shape = [P, TILES, E - 1]
            link(v.tensor_tensor(wide_as(shape), spread(iota_f[:, :], shape, 2),
                                 spread(first_f[:, 1:E], shape, 1), ALU.is_ge))
            link(v.tensor_reduce(need_f[:, :], wide_as(shape), AX, ALU.add))
            link(v.tensor_copy(tile_need[:, :], need_f[:, :]))
            link(v.tensor_scalar(tile_parity[:, :], tile_need[:, :], 1, None, ALU.bitwise_and))
            link(v.tensor_scalar(need_f[:, :], need_f[:, :], float(PIECES), float(PIECES), ALU.mult, ALU.add))
            v.tensor_copy(tile_need[:, :], need_f[:, :]).then_inc(routed, 1)
            dve.wait_ge(routed, 1)

            def xg_split(t, par):
                dve.wait_ge(xg_hi, t + 1)
                nc.vector.tensor_tensor(xgT[:, par, 1, :, :], HEADS[:, 0:D].rearrange("p (c n) -> p c n", c=DC),
                                        xgT[:, par, 0, :, :], ALU.subtract).then_inc(xg_ready, 1)

            xg_split(0, 0)

            def tile_step(t, par, u):
                if tile_on(t + 1):
                    xg_split(t + 1, 1 - par)
                if tile_on(t - 1):
                    for half in range(2):
                        dve.wait_ge(gT_hi, 2 * (t - 1) + half + 1)
                        chunk = slice(4 * half, 4 * half + 4)
                        nc.vector.tensor_tensor(gT[:, 1, chunk, :], banks[4 + half][:, :].rearrange("p (c n) -> p c n", c=4),
                                                gT[:, 0, chunk, :], ALU.subtract).then_inc(gT_ready, 1)
                if tile_on(t):
                    for half in range(2):
                        dve.wait_ge(h_done, 4 * t + 2 * half + 2)
                        dve.wait_ge(silu_done, 2 * t + half + 1)
                        wait(dve, gT_done, 2 * (t - 1) + half + 1)
                        nc.vector.tensor_tensor(g_sb[:, half, :], banks[2 * half + 1][:, :], act_h[:, half, :],
                                                ALU.mult).then_inc(g_done, 1)
                if tile_on(t - 1):
                    dve.wait_ge(y_done, t)
                    wait(dve, y_stored[1 - par], 16 * (u - 1 + par))
                    nc.vector.tensor_copy(y_sb[:, 1 - par, :], banks[6][:, 0:D]).then_inc(y_copied, 1)

            tile_steps(dve, tile_step)

            for i in range(TOK):
                dve.wait_ge(yk_gathered[i % 4], 32 * (i // 4 + 1))
                dve.wait_ge(xf_loaded[i % 4], 16 * (i // 4 + 1))
                x_i = xf[:, i % 4, :]
                v.scalar_tensor_tensor(x_i, yk[:, i % 4, 0, :], w_top[:, 0, i:i + 1], x_i,
                                       ALU.mult, ALU.add).then_inc(half_sum, 1)
                dve.wait_ge(half_sum, i + 1)
                v.scalar_tensor_tensor(x_i, yk[:, i % 4, 1, :], w_top[:, 1, i:i + 1], x_i,
                                       ALU.mult, ALU.add).then_inc(out_ready, 1)

        @block.tensor
        def _(pe):
            T = nc.tensor

            def project(n, bank, what, b, pair_in_batch):
                wait(pe, proj_free, n - 1)
                if what in ("q", "k"):
                    w, lo = (wq_s, NCTX) if what == "q" else (wk_s, 0)
                    cols = slice(pair_in_batch * P, (pair_in_batch + 1) * P)
                    for d in range(DC):
                        ins = split_product(PROJ[bank][:, 0:NKV - lo], lambda a: w[:, a, d, cols],
                                            lambda a: kvT[:, a, d, lo:NKV], d == 0, d == DC - 1)
                elif what[0] == "x":
                    d = what[2]
                    pe.wait_ge(z_ready, b + 1)
                    for n_tile in range(LNT):
                        rows = NCTX if n_tile == 0 else P
                        at = 0 if n_tile == 0 else NCTX + (n_tile - 1) * P
                        ins = T.transpose(PROJ[bank][:, at:at + rows], z[0:rows, n_tile, d * P:(d + 1) * P],
                                          ident[0:rows, 0:rows])
                else:
                    half, c = what[1], what[2]
                    rows = slice(c * P, c * P + KROWS[c])
                    for d in range(DC):
                        ins = split_product(PROJ[bank][0:KROWS[c], :], lambda a: kvT[:, a, d, rows],
                                            lambda a: wv_s[:, a, d, half * HALF:(half + 1) * HALF],
                                            d == 0, d == DC - 1)
                ins.then_inc(proj_done, 1)

            pe.sem_inc(wout_done, 1)
            pe.wait_ge(consts, 3)
            for item in FIRST_X:
                project(*item, 0)
            pe.wait_ge(kvT_ready, 2 * DC)
            for item in FIRST_QKV:
                pe.wait_ge(w_ready, 2 if item[2] in ("q", "k") else 3)
                project(*item, 0)

            def scores(b, q, j):
                s = b * PAIRS + q
                t = s * TPP + j
                c, h, par = j // 2, j % 2, q % 2
                if j == 0:
                    pe.wait_ge(qk_ready, 2 * (s + 1))
                wait(pe, exp_done, t - 1)
                rows = slice(h * DH, (h + 1) * DH)
                split_product(SCORE[j % 2][:, 0:NKV], lambda a: qT[rows, par, a, c * P:(c + 1) * P],
                              lambda a: kT[rows, par, a, :], True, True).then_inc(scores_done, 1)

            def transpose_probs(b, q, j):
                s = b * PAIRS + q
                pe.wait_ge(exp_done, s * TPP + j + 1)
                wait(pe, (pt_act, pt_dve)[j % 2], 2 * s + j // 2)
                for c in range(KC):
                    ins = T.transpose(TRANS[j % 2][:, c * P:(c + 1) * P], probs[:, q % 2, j, c * P:(c + 1) * P],
                                      ident[:, :])
                ins.then_inc(trans_done, 1)

            def probs_times_v(b, q, j):
                s = b * PAIRS + q
                bb, p = b + q // PAIRS, q % PAIRS
                h = j % 2
                if j == 0:
                    wait(pe, oT_ready, s)
                    pe.wait_ge(v_ready, 2 * KC * bb + (KC if p < PAIRS // 2 else 2 * KC))
                pe.wait_ge((pt_act, pt_dve)[j % 2], 2 * s + j // 2 + 1)
                cols = slice(p * P + h * DH, p * P + (h + 1) * DH)
                for c in range(KC):
                    ins = T.matmul(HEADS[:, j * DH:(j + 1) * DH], probsT[0:KROWS[c], j, c, :], v_sb[0:KROWS[c], c, cols],
                                   start=c == 0, stop=c == KC - 1)
                ins.then_inc(av_done, 1)

            def transpose_heads(s):
                pe.wait_ge(o_ready, s + 1)
                for c in range(QC):
                    ins = T.transpose(HEADS[:, (QC + c) * P:(QC + c + 1) * P], o_sb[:, c, :], ident[:, :])
                ins.then_inc(oT_done, 1)

            def output_projection(b, q):
                s = b * PAIRS + q
                bb, p = b + q // PAIRS, q % PAIRS
                pe.wait_ge(oT_ready, s + 1)
                if p == 0:
                    pe.wait_ge(x1_ready, 1 + bb)
                for c in range(QC):
                    ins = split_product(ACC[:, c * D:(c + 1) * D], lambda a: oT[:, a, c * P:(c + 1) * P],
                                        lambda a: wo_s[:, a, p, :], p == 0 and c == 0, p == PAIRS - 1 and c == QC - 1,
                                        skip_group_check=True)
                ins.then_inc(wout_done, 1)

            def step(b, q):
                s = b * PAIRS + q
                now, prev, last = stage_on(b, q, 0), stage_on(b, q, 1), stage_on(b, q, 2)
                items = step_items(b, q)
                if last:
                    transpose_heads(s - 2)
                for item in items:
                    if item[2] in ("q", "k"):
                        project(*item, (q + 1) % PAIRS)
                for j in range(TPP):
                    if now:
                        scores(b, q, j)
                    if prev:
                        transpose_probs(b, q - 1, j)
                        if j >= 1:
                            probs_times_v(b, q - 1, j - 1)
                    if last and j == 2:
                        output_projection(b, q - 2)
                if prev:
                    probs_times_v(b, q - 1, TPP - 1)
                for item in items:
                    if item[2] not in ("q", "k"):
                        project(*item, 0)
                        if item[2] == ("x", 0, DC - 1):
                            pe.wait_ge(kvT_ready, 2 * DC * item[3] + 2 * DC)

            pe.wait_ge(w_ready, 4)
            steps(pe, step)

            pe.wait_ge(xn_ready, TOK)

            def gate(i):
                for d in range(DC):
                    ins = T.matmul(SCORE[0][:, i * E:(i + 1) * E], xnT[:, i % 2, d, :], gate_sb[:, d, :],
                                   start=d == 0, stop=d == DC - 1)
                ins.then_inc(gates_done, 1)

            for i in range(TOK):
                wait(pe, xnT_ready, i - 1)
                for d in range(DC):
                    ins = T.transpose(PROJ[i % 2][:, d * P:(d + 1) * P], xn_all[:, i, d * P:(d + 1) * P], ident[:, :])
                ins.then_inc(xnT_done, 1)
                if i >= 1:
                    pe.wait_ge(xnT_ready, i)
                    gate(i - 1)
            pe.wait_ge(xnT_ready, TOK)
            gate(TOK - 1)
            pe.wait_ge(both_ready, 1)
            cols = both[:, :, :].rearrange("p i e -> p (i e)")
            T.matmul(SCORE[1][:, 0:TOK * E], tri[:, :], cols, start=True, stop=False, skip_group_check=True)
            for k in range(1, TOK):
                ins = T.matmul(SCORE[1][:, k * E:TOK * E], ones[:, :], cols[:, 0:(TOK - k) * E], start=False,
                               stop=k == TOK - 1, skip_group_check=True)
            ins.then_inc(ranks_done, 1)
            for i in range(TOK):
                ins = T.matmul(SCORE[1][:, TOK * E:(TOK + 1) * E], ones[:, :], both[:, i, :], start=False,
                               stop=i == TOK - 1, skip_group_check=True)
            ins.then_inc(ranks_done, 1)

            pe.wait_ge(routed, 1)

            def transpose_slots(t, par, u):
                pe.wait_ge(xg_loaded[par], 16 * (u + 1))
                wait(pe, xg_ready, t)
                for d in range(DC):
                    ins = T.transpose(HEADS[:, d * P:(d + 1) * P], xg[:, par, d * P:(d + 1) * P], ident[:, :])
                ins.then_inc(xg_trans, 1)

            def hidden(t, par, w):
                for half in range(2):
                    for m in range(2):
                        if m == 0:
                            wait(pe, silu_done, 2 * (t - 1) + half + 1)
                        else:
                            wait(pe, g_done, 2 * (t - 1) + half + 1)
                        for d in range(DC):
                            at = m * W3AT + d * F + half * FH
                            ins = split_product(banks[2 * half + m][:, :], lambda a: xgT[:, par, a, d, :],
                                                lambda a: W[:, w, a, at:at + FH], d == 0, d == DC - 1)
                        ins.then_inc(h_done, 1)

            def transpose_hidden(t):
                for half in range(2):
                    pe.wait_ge(g_done, 2 * t + half + 1)
                    wait(pe, gT_ready, 2 * (t - 1) + half + 1)
                    for n in range(4):
                        ins = T.transpose(banks[4 + half][:, n * P:(n + 1) * P], g_sb[:, half, n * P:(n + 1) * P],
                                          ident[:, :])
                    ins.then_inc(gT_done, 1)

            def expert_out(t, w):
                pe.wait_ge(gT_ready, 2 * (t + 1))
                wait(pe, y_copied, t)
                for n in range(FC):
                    at = W2AT + n * D
                    ins = split_product(banks[6][:, 0:D], lambda a: gT[:, a, n, :], lambda a: W[:, w, a, at:at + D],
                                        n == 0, n == FC - 1)
                ins.then_inc(y_done, 1)

            transpose_slots(0, 0, 0)

            def tile_step(t, par, u):
                if tile_on(t + 1):
                    transpose_slots(t + 1, 1 - par, u + par)
                if tile_on(t - 1):
                    transpose_hidden(t - 1)
                if tile_on(t):
                    need = pe.value_load(tile_need[0:1, bass.ds(t, 1)], min_val=PIECES, max_val=PIECES * E)
                    w = pe.value_load(tile_parity[0:1, bass.ds(t, 1)], min_val=0, max_val=1)
                    pe.wait_ge(pieces_ready, need)
                    pe.wait_ge(xg_ready, t + 1)
                    hidden(t, par, w)
                if tile_on(t - 1):
                    w = pe.value_load(tile_parity[0:1, bass.ds(t - 1, 1)], min_val=0, max_val=1)
                    expert_out(t - 1, w)

            tile_steps(pe, tile_step)


_INPUTS = ["x", "ctx_1024", "L0_xattn_ln_m_g", "L0_xattn_ln_m_b", "L0_xattn_ln_l_g", "L0_xattn_ln_l_b", "L0_xattn_Wq",
           "L0_xattn_Wkv", "L0_xattn_Wout", "L0_ffn_gate_w", "L0_ffn_w1", "L0_ffn_w3", "L0_ffn_w2"]


def kernel(**inputs):
    import numpy as np
    import concourse.bacc as bacc
    from concourse.bass_utils import run_bass_kernel_spmd

    nc = bacc.Bacc("TRN2", target_bir_lowering=False, num_devices=1)
    arrays, args = {}, []
    for name in _INPUTS:
        a = np.ascontiguousarray(inputs[name])
        arrays[f"in_{name}"] = a
        args.append(nc.dram_tensor(f"in_{name}", a.shape, mybir.dt.from_np(a.dtype), kind="ExternalInput").ap())
    shape = arrays["in_x"].shape
    args.append(nc.dram_tensor("out", shape, mybir.dt.float32, kind="ExternalOutput").ap())
    cross_attention_then_routed_ffn(nc, *args)
    r = run_bass_kernel_spmd(nc, [arrays], core_ids=[0])
    return r.results[0]["out"]
```

```python
import concourse.bass as bass
from concourse import mybir
from contextlib import ExitStack


def cross_attention_then_routed_ffn(
    nc: bass.Bass,
    x: bass.AP,
    context: bass.AP,
    ln_m_g: bass.AP,
    ln_m_b: bass.AP,
    ln_l_g: bass.AP,
    ln_l_b: bass.AP,
    Wq: bass.AP,
    Wkv: bass.AP,
    Wout: bass.AP,
    gate_w: bass.AP,
    w1: bass.AP,
    w3: bass.AP,
    w2: bass.AP,
    out: bass.AP,
):
    fp32, fp32r, bf16 = mybir.dt.float32, mybir.dt.float32r, mybir.dt.bfloat16
    i32, u32 = mybir.dt.int32, mybir.dt.uint32
    ALU = mybir.AluOpType
    ACT = mybir.ActivationFunctionType
    AX = mybir.AxisListType.X

    P = 128
    B, NQ, D = x.shape
    NCTX = context.shape[1]
    NKV = NCTX + NQ
    INNER = Wq.shape[1]
    DH = 64
    PAIRS = INNER // P
    DC = D // P
    QC = NQ // P
    KC = -(-NKV // P)
    KROWS = [min(P, NKV - P * c) for c in range(KC)]
    LNT = 1 + QC
    TPP = 2 * QC
    SCALE = DH ** -0.5
    HALF = INNER // 2
    EPS = 1e-5
    TOK = B * NQ // P
    E, _, F = w1.shape
    FC = F // P
    FH = F // 2
    TILES = (2 * B * NQ + E * P) // P
    SLOTS = TILES * P
    assert TILES % 2 == 0 and QC == 2 and DC == 2 and KC == 3 and PAIRS == 8
    PIECES = 6
    PW = DC * F // 2
    W3AT, W2AT, WCOLS = DC * F, 2 * DC * F, 2 * DC * F + FC * D

    x1_dram = nc.dram_tensor("x1_scratch", (TOK * P, D), fp32, kind="Internal").ap()
    xs_dram = nc.dram_tensor("slot_rows", (SLOTS, D), fp32, kind="Internal").ap()
    ys_dram = nc.dram_tensor("slot_outputs", (SLOTS, D), fp32, kind="Internal").ap()

    stack = ExitStack()
    sems = {}

    def sem(name):
        if name not in sems:
            sems[name] = stack.enter_context(nc.semaphore(name))
        return sems[name]

    with stack:
        def sb(name, shape, dt, ctx=stack):
            return ctx.enter_context(nc.sbuf_tensor(name, shape, dt))

        ident = sb("ident", [P, P], fp32)
        xn_all = sb("xn_all", [P, TOK, D], fp32)
        raw = sb("raw", [P, 2, PW], fp32)
        affine = sb("affine", [P, 4, DC], fp32)
        gate_sb = sb("gate_sb", [P, DC, E], fp32)
        w_top = sb("w_top", [P, 2, TOK], fp32)
        slot_of = sb("slot_of", [P, 2, TOK], u32)
        tile_parity = sb("tile_parity", [P, TILES], i32)
        tile_need = sb("tile_need", [P, TILES], i32)
        first_tile = sb("first_tile", [P, E], i32)

        attn = ExitStack()
        stage = sb("stage", [P, 4, 2048], fp32, attn)
        sb("stage_pad", [P, 4096], fp32, attn)
        wk_s = sb("wk_s", [P, 2, DC, INNER], fp32r, attn)
        wq_s = sb("wq_s", [P, 2, DC, INNER], fp32r, attn)
        wv_s = sb("wv_s", [P, 2, DC, INNER], fp32r, attn)
        wo_s = sb("wo_s", [P, 2, PAIRS, D], fp32r, attn)
        qT = sb("qT", [P, 2, 2, NQ], fp32r, attn)
        kT = sb("kT", [P, 2, 2, NKV], fp32r, attn)
        probs = sb("probs", [P, TPP, KC * P], fp32, attn)
        probsT = sb("probsT", [P, 2, 2, KC, NQ], fp32r, attn)
        v_s = sb("v_s", [P, 2, KC, INNER], fp32r, attn)
        kvT = sb("kvT", [P, 2, DC, NKV], fp32r, attn)
        xin_flat = sb("xin", [P, LNT * D], fp32, attn)
        xin = xin_flat[:, :].rearrange("p (n d) -> p n d", d=D)
        kvT_f = xin_flat[:, 0:DC * NKV].rearrange("p (c n) -> p c n", c=DC)
        z = sb("z", [P, LNT, D], fp32, attn)
        x1 = sb("x1", [P, QC, D], fp32, attn)
        oT = sb("oT", [P, 2, NQ], fp32r, attn)
        negmax = sb("negmax", [P, 2, TPP], fp32, attn)
        rowsum = sb("rowsum", [P, 2, TPP], fp32, attn)
        rinv = sb("rinv", [P, 2, TPP], fp32, attn)
        stats = sb("stats", [P, 2, LNT, 6], fp32, attn)
        mv = sb("mv", [P, 2, LNT, 2], fp32, attn)
        nve = sb("nve", [P, 2, LNT], fp32, attn)
        nt = sb("nt", [P, 2, LNT], fp32, attn)
        rstd = sb("rstd", [P, 2, LNT], fp32, attn)
        three_halves = sb("three_halves", [P, LNT], fp32, attn)
        attn.close()

        W = sb("W", [P, 2, 2, WCOLS], fp32r)
        zero = sb("zero", [P, D], fp32)
        xnT = sb("xnT", [P, 2, DC, P], fp32)
        lg = sb("lg", [P, TOK, E], fp32)
        mx = sb("mx", [P, TOK], fp32)
        ex = sb("ex", [P, TOK, E], fp32)
        top = sb("top", [P, TOK, 8], fp32)
        topi = sb("topi", [P, TOK, 8], u32)
        topf = sb("topf", [P, TOK, 8], fp32)
        pick = sb("pick", [P, 2, TOK, E], fp32)
        both = sb("both", [P, TOK, E], bf16)
        tri = sb("tri", [P, P], bf16)
        ones = sb("ones", [P, P], bf16)
        iota_i = sb("iota_i", [P, TILES], i32)
        iota_f = sb("iota_f", [P, TILES], fp32)
        count = sb("count", [P, E], fp32)
        wide = sb("wide", [P, TILES * E], fp32)
        before = sb("before", [P, E, E], fp32)
        tiles_of = sb("tiles_of", [P, E], fp32)
        first_f = sb("first_f", [P, E], fp32)
        base_f = sb("base_f", [P, E], fp32)
        slot_f = sb("slot_f", [P, TOK, E], fp32)
        slot_k = sb("slot_k", [P, 2, TOK], fp32)
        need_f = sb("need_f", [P, TILES], fp32)
        xg = sb("xg", [P, 2, D], fp32)
        xgT = sb("xgT", [P, 2, 2, DC, P], fp32r)
        act_h = sb("act_h", [P, 2, FH], fp32)
        g_sb = sb("g_sb", [P, 2, FH], fp32)
        gT = sb("gT", [P, 2, FC, P], fp32r)
        y_sb = sb("y_sb", [P, 2, D], fp32)
        yk = sb("yk", [P, 4, 2, D], fp32)
        xf = sb("xf", [P, 4, D], fp32)

        banks = [stack.enter_context(nc.psum_tensor(f"bank{n}", [P, 512], fp32)) for n in range(8)]
        PROJ, SCORE, TRANS, ACC, HEADS = banks[0:2], banks[2:4], banks[4:6], banks[6], banks[7]

        def wait(eng, s, value):
            if not (isinstance(value, int) and value <= 0):
                eng.wait_ge(s, value)

        def split_product(outp, stationary, moving, first, last, **kw):
            for n, (a, b) in enumerate(((0, 0), (0, 1), (1, 0))):
                ins = nc.tensor.matmul(outp, stationary(a), moving(b), start=first and n == 0,
                                       stop=last and n == 2, **kw)
            return ins

        ITEMS = [["q", "k"] for _ in range(PAIRS)]
        ITEMS[0] += [("v", 0, c) for c in range(1, KC)]
        for c in range(KC):
            ITEMS[1 + c] += [("v", 1, c)]
        ITEMS[6] += [("x", 0, d) for d in range(DC)]
        ITEMS[7] += [("v", 0, 0)]
        OFFSET = [sum(len(i) for i in ITEMS[:q]) for q in range(PAIRS + 1)]
        AHEAD = DC + 3
        assert OFFSET[PAIRS] % 2 == 0

        def step_items(b, q):
            b, q = b + q // PAIRS, q % PAIRS
            found = []
            for n, what in enumerate(ITEMS[q]):
                ahead = what[0] == "x" or what == ("v", 0, 0) or (q == PAIRS - 1 and what in ("q", "k"))
                if not (isinstance(b, int) and b + ahead >= B):
                    found.append((b * OFFSET[PAIRS] + (AHEAD + OFFSET[q] + n), (AHEAD + OFFSET[q] + n) % 2,
                                  what, b + 1 if ahead else b))
            return found

        FIRST_X = [(d, d % 2, ("x", 0, d), 0) for d in range(DC)]
        FIRST_QKV = [(DC + n, (DC + n) % 2, what, 0) for n, what in enumerate(["q", "k", ("v", 0, 0)])]

        head_outputs = [(slice(h * DH, (h + 1) * DH), HEADS[h * DH:(h + 1) * DH, h * NQ:(h + 1) * NQ])
                        for h in range(2)]

        def steps(eng, step):
            for q in range(3):
                step(0, q)
            with eng.Fori(0, B - 1) as b:
                for q in range(3, PAIRS + 3):
                    step(b, q)
            for q in range(3, PAIRS + 3):
                step(B - 1, q)

        def stage_on(b, q, lag):
            return not (isinstance(b, int) and not 0 <= b * PAIRS + q - lag < B * PAIRS)

        def tile_steps(eng, step):
            for t in range(3):
                step(t, t % 2, t // 2)
            with eng.Fori(1, TILES // 2 - 2) as i:
                step(2 * i + 1, 1, i)
                step(2 * i + 2, 0, i + 1)
            for t in range(TILES - 3, TILES + 1):
                step(t, t % 2, t // 2)

        def tile_on(t):
            return not (isinstance(t, int) and not 0 <= t < TILES)

        xin_loaded = sem("xin_loaded")
        xres_loaded, x1_stored = sem("xres_loaded"), sem("x1_stored")
        seeds_ready, newton_step = sem("seeds_ready"), sem("newton_step")
        small_loaded, stage_loaded = sem("small_loaded"), [sem(f"stage_loaded{n}") for n in range(4)]
        w_hi, w_ready = sem("w_hi"), sem("w_ready")
        consts, turns_taken = sem("consts"), sem("turns_taken")
        prep_step, fin_step, route_step = sem("prep_step"), sem("fin_step"), sem("route_step")
        z_ready, affine_done, kvT_hi, kvT_ready = sem("z_ready"), sem("affine_done"), sem("kvT_hi"), sem("kvT_ready")
        proj_done = sem("proj_done")
        qk_hi, qk_ready, v_hi, v_ready = sem("qk_hi"), sem("qk_ready"), sem("v_hi"), sem("v_ready")
        scores_done, max_done, exp_done = sem("scores_done"), sem("max_done"), sem("exp_done")
        trans_done, pT_hi, pT_ready, av_done = sem("trans_done"), sem("pT_hi"), sem("pT_ready"), sem("av_done")
        rinv_done, probs_ready = sem("rinv_done"), sem("probs_ready")
        oT_hi, oT_ready, wout_done = sem("oT_hi"), sem("oT_ready"), sem("wout_done")
        x1_ready, x1_seeds, xn_ready = sem("x1_ready"), sem("x1_seeds"), sem("xn_ready")
        raw_loaded, hi_loaded, pieces_ready = [sem(f"raw_loaded{n}") for n in range(2)], sem("hi_loaded"), sem("pieces_ready")
        zero_set, xs_zeroed, scattered = sem("zero_set"), sem("xs_zeroed"), sem("scattered")
        xnT_done, xnT_ready, gates_done, lg_done = sem("xnT_done"), sem("xnT_ready"), sem("gates_done"), sem("lg_done")
        gate_exp, routed, both_ready, ranks_done = sem("gate_exp"), sem("routed"), sem("both_ready"), sem("ranks_done")
        xg_loaded, xg_trans, xg_hi, xg_ready = [sem(f"xg_loaded{n}") for n in range(2)], sem("xg_trans"), sem("xg_hi"), sem("xg_ready")
        h_done, silu_done, g_done = sem("h_done"), sem("silu_done"), sem("g_done")
        gT_done, gT_hi, gT_ready = sem("gT_done"), sem("gT_hi"), sem("gT_ready")
        y_done, y_copied, y_stored = sem("y_done"), sem("y_copied"), [sem(f"y_stored{n}") for n in range(2)]
        yk_gathered, xf_loaded, half_sum, out_ready, out_stored = (
            [sem(f"yk_gathered{n}") for n in range(4)], [sem(f"xf_loaded{n}") for n in range(4)], sem("half_sum"),
            sem("out_ready"), [sem(f"out_stored{n}") for n in range(4)])

        block = stack.enter_context(nc.Block())

        x_rows = x.rearrange("b (c p) d -> b p c d", p=P)
        x1_rows = x1_dram.rearrange("(b c p) d -> b p c d", p=P, c=QC)
        xs_rows = xs_dram.rearrange("(t p) d -> t p d", p=P)
        ys_rows = ys_dram.rearrange("(t p) d -> t p d", p=P)
        out_rows = out.rearrange("b (c p) d -> (b c) p d", p=P)
        x1_tiles = x1_dram.rearrange("(t p) d -> t p d", p=P)

        def zero_fill_source():
            return zero[:, :].rearrange("p (o d) -> p o d", o=1).broadcast_to([P, TILES, D])

        def stage_of(n, w):
            return stage[:, n, :].rearrange("p (c m) -> p c m", c=w.shape[2])

        def raw_piece(e, n):
            if n < 2 * DC:
                return raw[:, n % 2, :], (w1, w3)[n // DC][e, (n % DC) * P:(n % DC + 1) * P, :]
            return (raw[:, n % 2, :].rearrange("p (c d) -> p c d", d=D),
                    w2[e, (n - 2 * DC) * FH:(n - 2 * DC + 1) * FH, :].rearrange("(c p) d -> p c d", p=P))

        @block.sync
        def _(sp):
            def load_xin(b):
                wait(sp, kvT_ready, DC * b)
                sp.dma_start(xin[0:NCTX, 0, :], context[b]).then_inc(xin_loaded, 16)
                sp.dma_start(xin[:, 1:LNT, :], x_rows[b]).then_inc(xin_loaded, 16)

            def load_xres(b):
                if not (isinstance(b, int) and b == 0):
                    sp.wait_ge(x1_stored, 16 * b)
                    sp.wait_ge(xn_ready, b)
                sp.dma_start(x1[:, :, :], x_rows[b]).then_inc(xres_loaded, 16)

            def store_x1(b):
                sp.wait_ge(x1_ready, 1 + b + 1)
                sp.dma_start(x1_rows[b], x1[:, :, :]).then_inc(x1_stored, 16)

            def load_raw(e):
                for n in range(PIECES):
                    wait(sp, pieces_ready, e * PIECES + n - 1)
                    sp.dma_start(*raw_piece(e, n)).then_inc(raw_loaded[n % 2], 16)

            sp.wait_ge(consts, 1)
            load_xin(0)
            sp.dma_start(stage[:, 0, :].rearrange("p (c n) -> p c n", c=DC),
                         Wkv[:, 0:INNER].rearrange("(c p) n -> p c n", p=P)).then_inc(stage_loaded[0], 16)
            sp.dma_start(stage[:, 1, :].rearrange("p (c n) -> p c n", c=DC),
                         Wq.rearrange("(c p) n -> p c n", p=P)).then_inc(stage_loaded[1], 16)
            sp.dma_start(stage[:, 2, :].rearrange("p (c n) -> p c n", c=DC),
                         Wkv[:, INNER:2 * INNER].rearrange("(c p) n -> p c n", p=P)).then_inc(stage_loaded[2], 16)
            sp.dma_start(stage[:, 3, :].rearrange("p (c n) -> p c n", c=PAIRS),
                         Wout.rearrange("(c p) n -> p c n", p=P)).then_inc(stage_loaded[3], 16)
            for n, vector in enumerate((ln_m_g, ln_m_b, ln_l_g, ln_l_b)):
                sp.dma_start(affine[:, n, :], vector.rearrange("(c p) -> p c", p=P), allow_slow_non_contiguous=True).then_inc(small_loaded, 16)
            sp.dma_start(gate_sb[:, :, :], gate_w.rearrange("(c p) e -> p c e", p=P)).then_inc(small_loaded, 16)
            load_xres(0)
            load_raw(0)
            load_xin(1)
            with sp.Fori(0, B - 2) as b:
                store_x1(b)
                load_xin(b + 2)
                load_xres(b + 1)
            store_x1(B - 2)
            load_xres(B - 1)
            store_x1(B - 1)

            sp.wait_ge(zero_set, 1)
            sp.dma_start(xs_dram.rearrange("(t p) d -> p t d", p=P), zero_fill_source()).then_inc(xs_zeroed, 16)

            with sp.Fori(1, E) as e:
                load_raw(e)

            for i in range(TOK):
                wait(sp, out_ready, i - 3)
                wait(sp, out_stored[i % 4], 16 * (i // 4))
                sp.dma_start(xf[:, i % 4, :], x1_tiles[i]).then_inc(xf_loaded[i % 4], 16)
                if i >= 2:
                    sp.wait_ge(out_ready, i - 1)
                    sp.dma_start(out_rows[i - 2], xf[:, (i - 2) % 4, :]).then_inc(out_stored[(i - 2) % 4], 16)
            for i in (TOK - 2, TOK - 1):
                sp.wait_ge(out_ready, i + 1)
                sp.dma_start(out_rows[i], xf[:, i % 4, :]).then_inc(out_stored[i % 4], 16)
            for s in out_stored:
                sp.wait_ge(s, 16 * TOK // 4)
            sp.wait_ge(x1_stored, 16 * B)

        @block.gpsimd
        def _(pool):
            nc.gpsimd.memset(xin[:, 0, :], 0.0).then_inc(consts, 1)
            nc.gpsimd.memset(ident[:, :], 0.0).then_inc(consts, 1)
            pool.wait_ge(consts, 2)
            nc.gpsimd.affine_select(out=ident[:, :], in_=ident[:, :], compare_op=ALU.not_equal, fill=1.0,
                                    base=0, pattern=[[-1, P]], channel_multiplier=1).then_inc(consts, 1)
            nc.gpsimd.memset(probs[:, :, NKV:KC * P], 0.0).then_inc(consts, 1)

            def split_expert(e):
                for n, w in enumerate((w1, w3)):
                    pool.dma_start(W[:, e % 2, 0, n * W3AT:(n + 1) * W3AT].rearrange("p (c f) -> p c f", c=DC),
                                   w[e].rearrange("(c p) f -> p c f", p=P)).then_inc(hi_loaded, 16)
                pool.dma_start(W[:, e % 2, 0, W2AT:WCOLS].rearrange("p (c d) -> p c d", c=FC),
                               w2[e].rearrange("(c p) d -> p c d", p=P)).then_inc(hi_loaded, 16)
                pool.wait_ge(hi_loaded, 48 * (e + 1))
                for n in range(PIECES):
                    k = e * PIECES + n
                    cols = slice(n * PW, (n + 1) * PW)
                    pool.wait_ge(raw_loaded[n % 2], 16 * (k // 2 + 1))
                    nc.gpsimd.tensor_tensor(W[:, e % 2, 1, cols], raw[:, n % 2, :], W[:, e % 2, 0, cols],
                                            ALU.subtract).then_inc(pieces_ready, 1)

            NEWTON = 12
            CHAIN = NEWTON + 1

            def newton(link, k, n):
                y, t = rstd[:, k, 0:n], nt[:, k, 0:n]
                for _ in range(3):
                    link(nc.gpsimd.tensor_tensor(t, y, y, ALU.mult))
                    link(nc.gpsimd.tensor_tensor(t, t, nve[:, k, 0:n], ALU.mult))
                    link(nc.gpsimd.tensor_tensor(t, t, three_halves[:, 0:n], ALU.add))
                    link(nc.gpsimd.tensor_tensor(y, y, t, ALU.mult))

            def pool_chain(start):
                at = [0]

                def link(ins):
                    at[0] += 1
                    ins.then_inc(newton_step, 1)
                    pool.wait_ge(newton_step, start + at[0])
                return link

            def centred(outp, inp, k, n, op):
                by = mv[:, k, 0:n, 0] if op == ALU.subtract else rstd[:, k, 0:n]
                return nc.gpsimd.tensor_tensor(outp, inp, by.unsqueeze(2).broadcast_to([P, n, D]), op)

            def prepare_rstd(b, start):
                pool.wait_ge(seeds_ready, b + 1)
                newton(pool_chain(start), 0, LNT)

            def prepare_z(b, start):
                link = pool_chain(start + NEWTON)
                link(centred(z[:, :, :], xin, 0, LNT, ALU.subtract))
                centred(z[:, :, :], z[:, :, :], 0, LNT, ALU.mult).then_inc(z_ready, 1)

            def finish_batch(b, start):
                link = pool_chain(start)
                pool.wait_ge(x1_seeds, b + 1)
                newton(link, 1, QC)
                rows = xn_all[:, bass.ds(b * QC, QC), :]
                pool.sem_inc(turns_taken, 1)
                link(centred(rows, x1[:, :, :], 1, QC, ALU.subtract))
                pool.sem_inc(turns_taken, 1)
                centred(rows, rows, 1, QC, ALU.mult).then_inc(xn_ready, 1)

            def step(b, q):
                s = b * PAIRS + q
                more = not (isinstance(b, int) and b == B - 1)
                if stage_on(b, q, 0):
                    for j in range(TPP):
                        pool.wait_ge(rinv_done, 2 * s + j // 2 + 1)
                        nc.gpsimd.tensor_tensor(probs[:, j, 0:NKV], probs[:, j, 0:NKV],
                                                rinv[:, q % 2, j:j + 1].broadcast_to([P, NKV]),
                                                ALU.mult).then_inc(probs_ready, 1)
                if q == 4 and more:
                    prepare_rstd(b + 1, CHAIN * (2 * b + 1))
                if q == 5 and more:
                    prepare_z(b + 1, CHAIN * (2 * b + 1))
                if q == PAIRS + 2:
                    finish_batch(b, CHAIN * (2 * b + (2 if more else 1)))

            nc.gpsimd.memset(three_halves[:, :], 1.5).then_inc(consts, 1)
            pool.wait_ge(consts, 5)
            prepare_rstd(0, 0)
            prepare_z(0, 0)
            pool.wait_ge(w_ready, 4)
            split_expert(0)
            steps(pool, step)

            pool.wait_ge(xn_ready, B)
            nc.gpsimd.memset(zero[:, :], 0.0).then_inc(zero_set, 1)
            nc.gpsimd.iota(iota_i[:, :], pattern=[[1, TILES]], base=0, channel_multiplier=0).then_inc(consts, 1)
            nc.gpsimd.memset(ones[:, :], 1.0).then_inc(consts, 1)
            nc.gpsimd.memset(before[:, :, :], 1.0).then_inc(consts, 1)
            pool.wait_ge(consts, 8)
            nc.gpsimd.affine_select(out=tri[:, :], in_=ones[:, :], compare_op=ALU.is_gt, fill=0.0, base=0,
                                    pattern=[[1, P]], channel_multiplier=-1).then_inc(consts, 1)
            nc.gpsimd.affine_select(out=before[:, :, :], in_=before[:, :, :], compare_op=ALU.is_gt, fill=0.0,
                                    base=0, pattern=[[1, E], [-1, E]], channel_multiplier=0).then_inc(consts, 1)

            pool.wait_ge(xs_zeroed, 16)
            pool.wait_ge(routed, 1)
            for i in range(TOK):
                for k in range(2):
                    nc.gpsimd.indirect_dma_start(
                        out=xs_dram, out_offset=bass.IndirectOffsetOnAxis(ap=slot_of[:, k, i:i + 1], axis=0),
                        in_=xn_all[:, i, :], in_offset=None).then_inc(scattered, 16)
            for e in range(1, E):
                if e >= 2:
                    start = pool.value_load(first_tile[0:1, e - 1:e], min_val=0, max_val=TILES)
                    pool.wait_ge(y_done, start)
                    pool.sem_inc(turns_taken, 1)
                split_expert(e)

            for s in y_stored:
                pool.wait_ge(s, 16 * TILES // 2)
            for i in range(TOK):
                wait(pool, out_ready, i - 3)
                for k in range(2):
                    nc.gpsimd.indirect_dma_start(
                        out=yk[:, i % 4, k, :], out_offset=None, in_=ys_dram,
                        in_offset=bass.IndirectOffsetOnAxis(ap=slot_of[:, k, i:i + 1], axis=0)).then_inc(yk_gathered[i % 4], 16)

        @block.scalar
        def _(act):
            def proj_hi(n, bank, what, b, par):
                if what[0] == "x":
                    act.wait_ge(affine_done, 2 * DC * b + 2 * (what[2] + 1))
                    nc.scalar.activation(kvT[:, 0, what[2], :], kvT_f[:, what[2], :], ACT.Copy).then_inc(kvT_hi, 1)
                    return
                act.wait_ge(proj_done, n + 1)
                if what == "q":
                    nc.scalar.activation(qT[:, par, 0, :], PROJ[bank][:, 0:NQ], ACT.Copy, scale=SCALE).then_inc(qk_hi, 1)
                elif what[0] == "v":
                    half, c = what[1], what[2]
                    nc.scalar.activation(v_s[0:KROWS[c], 0, c, half * HALF:(half + 1) * HALF],
                                         PROJ[bank][0:KROWS[c], :], ACT.Copy).then_inc(v_hi, 1)
                else:
                    nc.scalar.activation(kT[:, par, 0, :], PROJ[bank][:, 0:NKV], ACT.Copy).then_inc(qk_hi, 1)

            for item in FIRST_X:
                proj_hi(*item, 0)
            for n, w in enumerate((wk_s, wq_s, wv_s, wo_s)):
                act.wait_ge(stage_loaded[n], 16)
                nc.scalar.activation(w[:, 0, :, :], stage_of(n, w), ACT.Copy).then_inc(w_hi, 1)
            for item in FIRST_QKV:
                proj_hi(*item, 0)
            act.wait_ge(consts, 4)

            def step(b, q):
                s = b * PAIRS + q
                items = step_items(b, q)
                for j in range(TPP):
                    if stage_on(b, q, 1):
                        t, h = (s - 1) * TPP + j, j // 2
                        act.wait_ge(trans_done, t + 1)
                        wait(act, av_done, 2 * (s - 2) + h + 1)
                        nc.scalar.activation(probsT[:, h, 0, :, (j % 2) * P:(j % 2 + 1) * P],
                                             TRANS[j % 2][:, 0:KC * P].rearrange("p (c n) -> p c n", c=KC),
                                             ACT.Copy).then_inc(pT_hi, 1)
                    if stage_on(b, q, 0):
                        t = s * TPP + j
                        act.wait_ge(max_done, t + 1)
                        wait(act, trans_done, t - 3)
                        nc.scalar.activation(probs[:, j, 0:NKV], SCORE[j % 2][:, 0:NKV], ACT.Exp,
                                             bias=negmax[:, q % 2, j:j + 1],
                                             accum_out=rowsum[:, q % 2, j:j + 1]).then_inc(exp_done, 1)
                    if j % 2 == 1:
                        for item in items[j // 2:j // 2 + 1]:
                            proj_hi(*item, (q + 1) % 2)
                if stage_on(b, q, 1):
                    act.wait_ge(av_done, 2 * s)
                    wait(act, wout_done, 1 + s - 1)
                    for rows, src in head_outputs:
                        nc.scalar.activation(oT[rows, 0, :], src, ACT.Copy).then_inc(oT_hi, 1)
                for item in items[2:]:
                    proj_hi(*item, 0)

            steps(act, step)

            act.wait_ge(lg_done, 1)
            nc.scalar.activation(ex[:, :, :], lg[:, :, :], ACT.Exp).then_inc(gate_exp, 1)

            def xg_split(t, par):
                act.wait_ge(xg_trans, t + 1)
                wait(act, h_done, 4 * (t - 1))
                nc.scalar.activation(xgT[:, par, 0, :, :], HEADS[:, 0:D].rearrange("p (c n) -> p c n", c=DC),
                                     ACT.Copy).then_inc(xg_hi, 1)

            def load_slots(t, par):
                if tile_on(t):
                    wait(act, xg_trans, t - 1)
                    act.dma_start(xg[:, par, :], xs_rows[t]).then_inc(xg_loaded[par], 16)

            def store_y(t, par):
                act.wait_ge(y_copied, t + 1)
                act.dma_start(ys_rows[t], y_sb[:, par, :]).then_inc(y_stored[par], 16)

            act.wait_ge(scattered, 32 * TOK)
            load_slots(0, 0)
            load_slots(1, 1)
            xg_split(0, 0)

            def tile_step(t, par, u):
                if not (isinstance(t, int) and t < 2):
                    store_y(t - 2, par)
                if not (isinstance(t, int) and t + 2 >= TILES):
                    load_slots(t + 2, par)
                if tile_on(t + 1):
                    xg_split(t + 1, 1 - par)
                if tile_on(t - 1):
                    for half in range(2):
                        act.wait_ge(gT_done, 2 * (t - 1) + half + 1)
                        wait(act, y_done, t - 1)
                        nc.scalar.activation(gT[:, 0, 4 * half:4 * half + 4, :],
                                             banks[4 + half][:, :].rearrange("p (c n) -> p c n", c=4),
                                             ACT.Copy).then_inc(gT_hi, 1)
                if tile_on(t):
                    for half in range(2):
                        act.wait_ge(h_done, 4 * t + 2 * half + 1)
                        wait(act, g_done, 2 * (t - 1) + half + 1)
                        nc.scalar.activation(act_h[:, half, :], banks[2 * half][:, :], ACT.Silu).then_inc(silu_done, 1)

            tile_steps(act, tile_step)
            store_y(TILES - 1, 1)

        @block.vector
        def _(dve):
            def chain(s, start):
                at = [0]

                def link(ins):
                    at[0] += 1
                    ins.then_inc(s, 1)
                    dve.wait_ge(s, start + at[0])
                return link, at

            def seed(stage, k, tiles, start, done):
                n = len(tiles)
                bits = nt[:, k, 0:n].bitcast(i32)
                s = (prep_step, fin_step)[k]
                if stage:
                    dve.wait_ge(s, start + stage)
                if stage == 0:
                    for m, tile in enumerate(tiles):
                        ins = nc.vector.bn_stats(stats[:, k, m, :], tile)
                elif stage == 1:
                    dve.sem_inc(turns_taken, 1)
                    for m in range(n):
                        ins = nc.vector.bn_aggr(mv[:, k, m, :], stats[:, k, m, :])
                elif stage == 2:
                    once = 1 if k == 0 else n
                    ins = nc.vector.tensor_scalar(nve[:, k, 0:once], mv[:, k, 0:once, 1], EPS, -0.5, ALU.add, ALU.mult)
                    if once < n:
                        ins = nc.vector.tensor_scalar(nve[:, k, once:n], mv[:, k, once:n, 1], -0.5 * (1 + EPS),
                                                      -0.5 * EPS * EPS, ALU.mult, ALU.add)
                elif stage == 3:
                    ins = nc.vector.tensor_scalar(bits, nve[:, k, 0:n].bitcast(i32), 1, None, ALU.logical_shift_right)
                else:
                    ins = nc.vector.tensor_scalar(rstd[:, k, 0:n].bitcast(i32), bits, -1.0, float(0x5F3759DF + 0x3FC00000),
                                                  ALU.mult, ALU.add)
                ins.then_inc(done if stage == 4 else s, 1)

            def prepare(b, stage):
                if stage == 0:
                    dve.wait_ge(xin_loaded, 32 * (b + 1))
                seed(stage, 0, [xin[:, n, :] for n in range(LNT)], 4 * b, seeds_ready)

            def add_attention(b):
                dve.wait_ge(wout_done, 1 + PAIRS * (b + 1))
                dve.wait_ge(xres_loaded, 16 * (b + 1))
                nc.vector.tensor_tensor(x1[:, :, :], ACC[:, :].rearrange("p (c d) -> p c d", c=QC), x1[:, :, :],
                                        ALU.add).then_inc(x1_ready, 1)

            def finish_batch(b, stage):
                if stage == 0:
                    dve.wait_ge(x1_ready, 1 + b + 1)
                seed(stage, 1, [x1[:, n, :] for n in range(QC)], 4 * b, x1_seeds)

            def evacuate(n, bank, what, b, pair, par):
                src = PROJ[bank]
                if what == "q":
                    dve.wait_ge(qk_hi, 2 * pair + 1)
                    nc.vector.scalar_tensor_tensor(qT[:, par, 1, :], src[:, 0:NQ], SCALE, qT[:, par, 0, :],
                                                   ALU.mult, ALU.subtract).then_inc(qk_ready, 1)
                elif what == "k":
                    dve.wait_ge(qk_hi, 2 * pair + 2)
                    nc.vector.tensor_tensor(kT[:, par, 1, :], src[:, 0:NKV], kT[:, par, 0, :],
                                            ALU.subtract).then_inc(qk_ready, 1)
                elif what[0] == "x":
                    d = what[2]
                    dve.wait_ge(proj_done, n + 1)
                    for lo, hi, g in ((0, NCTX, 0), (NCTX, NKV, 2)):
                        nc.vector.tensor_scalar(kvT_f[:, d, lo:hi], src[:, lo:hi], affine[:, g, d:d + 1],
                                                affine[:, g + 1, d:d + 1], ALU.mult, ALU.add).then_inc(affine_done, 1)
                    if d == DC - 1:
                        for m in range(DC):
                            dve.wait_ge(kvT_hi, DC * b + m + 1)
                            nc.vector.tensor_tensor(kvT[:, 1, m, :], kvT_f[:, m, :], kvT[:, 0, m, :],
                                                    ALU.subtract).then_inc(kvT_ready, 1)
                else:
                    half, c = what[1], what[2]
                    dve.wait_ge(v_hi, 2 * KC * b + KC * half + c + 1)
                    cols = slice(half * HALF, (half + 1) * HALF)
                    nc.vector.tensor_tensor(v_s[0:KROWS[c], 1, c, cols], src[0:KROWS[c], :], v_s[0:KROWS[c], 0, c, cols],
                                            ALU.subtract).then_inc(v_ready, 1)

            for stage in range(5):
                prepare(0, stage)
            dve.sem_inc(x1_ready, 1)
            dve.wait_ge(small_loaded, 16 * 5)
            for item in FIRST_X:
                evacuate(*item, 0, 0)
            for n, w in enumerate((wk_s, wq_s, wv_s, wo_s)):
                dve.wait_ge(w_hi, n + 1)
                nc.vector.tensor_tensor(w[:, 1, :, :], stage_of(n, w), w[:, 0, :, :], ALU.subtract).then_inc(w_ready, 1)
            for item in FIRST_QKV:
                evacuate(*item, 0, 0)

            def reciprocal_sums(s, h, par):
                dve.wait_ge(exp_done, TPP * s + 2 * h + 2)
                wait(dve, probs_ready, TPP * (s - 2) + 2 * h + 2)
                nc.vector.reciprocal(rinv[:, par, 2 * h:2 * h + 2], rowsum[:, par, 2 * h:2 * h + 2]).then_inc(rinv_done, 1)

            def step(b, q):
                s = b * PAIRS + q
                items = step_items(b, q)
                more = not (isinstance(b, int) and b == B - 1)
                for j in range(TPP):
                    if stage_on(b, q, 0):
                        dve.wait_ge(scores_done, s * TPP + j + 1)
                        nc.vector.tensor_reduce(negmax[:, q % 2, j:j + 1], SCORE[j % 2][:, 0:NKV], AX, ALU.max,
                                                negate=True).then_inc(max_done, 1)
                    if stage_on(b, q, 1):
                        t, h = (s - 1) * TPP + j, j // 2
                        cols = slice((j % 2) * P, (j % 2 + 1) * P)
                        dve.wait_ge(pT_hi, t + 1)
                        nc.vector.tensor_tensor(probsT[:, h, 1, :, cols],
                                                TRANS[j % 2][:, 0:KC * P].rearrange("p (c n) -> p c n", c=KC),
                                                probsT[:, h, 0, :, cols], ALU.subtract).then_inc(pT_ready, 1)
                    if j % 2 == 1:
                        for item in items[j // 2:j // 2 + 1]:
                            evacuate(*item, s + 1, (q + 1) % 2)
                    if j == 2 and stage_on(b, q, 0):
                        reciprocal_sums(s, 0, q % 2)
                    if q == 3 and more:
                        prepare(b + 1, j)
                    if q == 4 and more and j == 0:
                        prepare(b + 1, 4)
                    if q == PAIRS + 2:
                        finish_batch(b, 1 + j)
                if stage_on(b, q, 0):
                    reciprocal_sums(s, 1, q % 2)
                if stage_on(b, q, 1):
                    dve.wait_ge(oT_hi, 2 * s)
                    for rows, src in head_outputs:
                        nc.vector.tensor_tensor(oT[rows, 1, :], src, oT[rows, 0, :], ALU.subtract).then_inc(oT_ready, 1)
                for item in items[2:]:
                    evacuate(*item, 0, 0)
                if q == PAIRS + 1:
                    add_attention(b)
                    finish_batch(b, 0)

            steps(dve, step)

            dve.wait_ge(xn_ready, B)
            for i in range(TOK):
                dve.wait_ge(xnT_done, i + 1)
                wait(dve, gates_done, i - 1)
                nc.vector.tensor_copy(xnT[:, i % 2, :, :], PROJ[i % 2][:, 0:D].rearrange("p (c n) -> p c n", c=DC)
                                      ).then_inc(xnT_ready, 1)
            link, _ = chain(route_step, 0)
            dve.wait_ge(gates_done, TOK)
            dve.wait_ge(consts, 10)
            v = nc.vector

            def wide_as(shape):
                n = 1
                for m in shape[1:]:
                    n *= m
                names = "abc"[:len(shape) - 1]
                sizes = dict(zip(names, shape[1:]))
                return wide[:, 0:n].rearrange(f"p ({' '.join(names)}) -> p {' '.join(names)}", **sizes)

            def spread(ap, shape, at):
                return ap.unsqueeze(at).broadcast_to(shape)

            TE = [P, TOK, E]
            gates = SCORE[0][:, 0:TOK * E].rearrange("p (i e) -> p i e", e=E)
            link(v.tensor_reduce(mx[:, :], gates, AX, ALU.max))
            v.tensor_tensor(lg[:, :, :], gates, spread(mx[:, :], TE, 2), ALU.subtract).then_inc(lg_done, 1)
            dve.wait_ge(gate_exp, 1)
            link(v.tensor_reduce(mx[:, :], ex[:, :, :], AX, ALU.add))
            link(v.reciprocal(mx[:, :], mx[:, :]))
            link(v.tensor_tensor(ex[:, :, :], ex[:, :, :], spread(mx[:, :], TE, 2), ALU.mult))
            for i in range(TOK):
                ins = v.max(top[:, i, :], ex[:, i, :])
            link(ins)
            for i in range(TOK):
                ins = v.max_index(topi[:, i, :], top[:, i, :], ex[:, i, :])
            link(ins)
            link(v.tensor_copy(topf[:, :, 0:2], topi[:, :, 0:2]))
            link(v.tensor_copy(iota_f[:, :], iota_i[:, :]))
            for k in range(2):
                link(v.tensor_tensor(pick[:, k, :, :], spread(topf[:, :, k], TE, 2),
                                     spread(iota_f[:, 0:E], TE, 1), ALU.is_equal))
            v.tensor_tensor(both[:, :, :], pick[:, 0, :, :], pick[:, 1, :, :], ALU.add).then_inc(both_ready, 1)
            link(v.tensor_tensor(mx[:, :], top[:, :, 0], top[:, :, 1], ALU.add))
            link(v.reciprocal(mx[:, :], mx[:, :]))
            link(v.tensor_tensor(w_top[:, :, :], top[:, :, 0:2].rearrange("p i k -> p k i"),
                                 spread(mx[:, :], [P, 2, TOK], 1), ALU.mult))
            dve.wait_ge(ranks_done, 2)
            link(v.tensor_copy(count[:, :], SCORE[1][:, TOK * E:TOK * E + E]))
            steps_of = TOK - 1
            link(v.tensor_scalar(need_f[:, 0:steps_of], iota_f[:, 1:TOK], float(P), None, ALU.mult))
            shape = [P, E, steps_of]
            link(v.tensor_tensor(wide_as(shape), spread(count[:, :], shape, 2),
                                 spread(need_f[:, 0:steps_of], shape, 1), ALU.is_gt))
            link(v.tensor_reduce(tiles_of[:, :], wide_as(shape), AX, ALU.add))
            link(v.tensor_scalar(tiles_of[:, :], tiles_of[:, :], 1.0, None, ALU.add))
            shape = [P, E, E]
            link(v.tensor_tensor(wide_as(shape), before[:, :, :], spread(tiles_of[:, :], shape, 1), ALU.mult))
            link(v.tensor_reduce(first_f[:, :], wide_as(shape), AX, ALU.add))
            link(v.tensor_copy(first_tile[:, :], first_f[:, :]))
            link(v.tensor_scalar(base_f[:, :], first_f[:, :], float(P), None, ALU.mult))
            link(v.tensor_tensor(slot_f[:, :, :], SCORE[1][:, 0:TOK * E].rearrange("p (i e) -> p i e", e=E),
                                 spread(base_f[:, :], TE, 1), ALU.add))
            for k in range(2):
                link(v.tensor_tensor(wide_as(TE), pick[:, k, :, :], slot_f[:, :, :], ALU.mult))
                link(v.tensor_reduce(slot_k[:, k, :], wide_as(TE), AX, ALU.add))
            link(v.tensor_copy(slot_of[:, :, :], slot_k[:, :, :]))
            shape = [P, TILES, E - 1]
            link(v.tensor_tensor(wide_as(shape), spread(iota_f[:, :], shape, 2),
                                 spread(first_f[:, 1:E], shape, 1), ALU.is_ge))
            link(v.tensor_reduce(need_f[:, :], wide_as(shape), AX, ALU.add))
            link(v.tensor_copy(tile_need[:, :], need_f[:, :]))
            link(v.tensor_scalar(tile_parity[:, :], tile_need[:, :], 1, None, ALU.bitwise_and))
            link(v.tensor_scalar(need_f[:, :], need_f[:, :], float(PIECES), float(PIECES), ALU.mult, ALU.add))
            v.tensor_copy(tile_need[:, :], need_f[:, :]).then_inc(routed, 1)
            dve.wait_ge(routed, 1)

            def xg_split(t, par):
                dve.wait_ge(xg_hi, t + 1)
                nc.vector.tensor_tensor(xgT[:, par, 1, :, :], HEADS[:, 0:D].rearrange("p (c n) -> p c n", c=DC),
                                        xgT[:, par, 0, :, :], ALU.subtract).then_inc(xg_ready, 1)

            xg_split(0, 0)

            def tile_step(t, par, u):
                if tile_on(t + 1):
                    xg_split(t + 1, 1 - par)
                if tile_on(t - 1):
                    for half in range(2):
                        dve.wait_ge(gT_hi, 2 * (t - 1) + half + 1)
                        chunk = slice(4 * half, 4 * half + 4)
                        nc.vector.tensor_tensor(gT[:, 1, chunk, :], banks[4 + half][:, :].rearrange("p (c n) -> p c n", c=4),
                                                gT[:, 0, chunk, :], ALU.subtract).then_inc(gT_ready, 1)
                if tile_on(t):
                    for half in range(2):
                        dve.wait_ge(h_done, 4 * t + 2 * half + 2)
                        dve.wait_ge(silu_done, 2 * t + half + 1)
                        wait(dve, gT_done, 2 * (t - 1) + half + 1)
                        nc.vector.tensor_tensor(g_sb[:, half, :], banks[2 * half + 1][:, :], act_h[:, half, :],
                                                ALU.mult).then_inc(g_done, 1)
                if tile_on(t - 1):
                    dve.wait_ge(y_done, t)
                    wait(dve, y_stored[1 - par], 16 * (u - 1 + par))
                    nc.vector.tensor_copy(y_sb[:, 1 - par, :], banks[6][:, 0:D]).then_inc(y_copied, 1)

            tile_steps(dve, tile_step)

            for i in range(TOK):
                dve.wait_ge(yk_gathered[i % 4], 32 * (i // 4 + 1))
                dve.wait_ge(xf_loaded[i % 4], 16 * (i // 4 + 1))
                x_i = xf[:, i % 4, :]
                v.scalar_tensor_tensor(x_i, yk[:, i % 4, 0, :], w_top[:, 0, i:i + 1], x_i,
                                       ALU.mult, ALU.add).then_inc(half_sum, 1)
                dve.wait_ge(half_sum, i + 1)
                v.scalar_tensor_tensor(x_i, yk[:, i % 4, 1, :], w_top[:, 1, i:i + 1], x_i,
                                       ALU.mult, ALU.add).then_inc(out_ready, 1)

        @block.tensor
        def _(pe):
            T = nc.tensor

            def copied(what, b, pair):
                if what in ("q", "k"):
                    return qk_ready, 2 * pair + 1 + (what == "k")
                if what[0] == "x":
                    return kvT_ready, DC * b + what[2] + 1
                return v_ready, 2 * KC * b + KC * what[1] + what[2] + 1

            def project(n, bank, what, b, pair_in_batch, left):
                if left:
                    pe.wait_ge(*left)
                if what in ("q", "k"):
                    w, lo = (wq_s, NCTX) if what == "q" else (wk_s, 0)
                    cols = slice(pair_in_batch * P, (pair_in_batch + 1) * P)
                    for d in range(DC):
                        ins = split_product(PROJ[bank][:, 0:NKV - lo], lambda a: w[:, a, d, cols],
                                            lambda a: kvT[:, a, d, lo:NKV], d == 0, d == DC - 1)
                elif what[0] == "x":
                    d = what[2]
                    pe.wait_ge(z_ready, b + 1)
                    for n_tile in range(LNT):
                        rows = NCTX if n_tile == 0 else P
                        at = 0 if n_tile == 0 else NCTX + (n_tile - 1) * P
                        ins = T.transpose(PROJ[bank][:, at:at + rows], z[0:rows, n_tile, d * P:(d + 1) * P],
                                          ident[0:rows, 0:rows])
                else:
                    half, c = what[1], what[2]
                    rows = slice(c * P, c * P + KROWS[c])
                    for d in range(DC):
                        ins = split_product(PROJ[bank][0:KROWS[c], :], lambda a: kvT[:, a, d, rows],
                                            lambda a: wv_s[:, a, d, half * HALF:(half + 1) * HALF],
                                            d == 0, d == DC - 1)
                ins.then_inc(proj_done, 1)

            pe.sem_inc(wout_done, 1)
            pe.wait_ge(consts, 3)
            firsts = [copied(item[2], 0, 0) for item in FIRST_X + FIRST_QKV]
            for item in FIRST_X:
                project(*item, 0, None)
            pe.wait_ge(kvT_ready, DC)
            for n, item in enumerate(FIRST_QKV):
                pe.wait_ge(w_ready, {"q": 2, "k": 2}.get(item[2], 3))
                project(*item, 0, firsts[n])

            def scores(b, q, j):
                s = b * PAIRS + q
                t = s * TPP + j
                h, c, par = j // 2, j % 2, q % 2
                if j == 0:
                    pe.wait_ge(qk_ready, 2 * (s + 1))
                wait(pe, exp_done, t - 1)
                rows = slice(h * DH, (h + 1) * DH)
                split_product(SCORE[j % 2][:, 0:NKV], lambda a: qT[rows, par, a, c * P:(c + 1) * P],
                              lambda a: kT[rows, par, a, :], True, True).then_inc(scores_done, 1)

            def transpose_probs(b, q, j):
                s = b * PAIRS + q
                pe.wait_ge(probs_ready, s * TPP + j + 1)
                wait(pe, pT_ready, s * TPP + j - 1)
                for c in range(KC):
                    ins = T.transpose(TRANS[j % 2][:, c * P:(c + 1) * P], probs[:, j, c * P:(c + 1) * P],
                                      ident[:, :])
                ins.then_inc(trans_done, 1)

            def v_times_probs(b, q, h):
                s = b * PAIRS + q
                bb, p = b + q // PAIRS, q % PAIRS
                if h == 0:
                    wait(pe, oT_ready, 2 * s)
                    pe.wait_ge(v_ready, 2 * KC * bb + (KC if p < PAIRS // 2 else 2 * KC))
                pe.wait_ge(pT_ready, s * TPP + 2 * h + 2)
                cols = slice(p * P, (p + 1) * P)
                for c in range(KC):
                    ins = split_product(HEADS[:, h * NQ:(h + 1) * NQ], lambda a: v_s[0:KROWS[c], a, c, cols],
                                        lambda a: probsT[0:KROWS[c], h, a, c, :], c == 0, c == KC - 1)
                ins.then_inc(av_done, 1)

            def output_projection(b, q):
                s = b * PAIRS + q
                bb, p = b + q // PAIRS, q % PAIRS
                pe.wait_ge(oT_ready, 2 * s + 2)
                if p == 0:
                    pe.wait_ge(x1_ready, 1 + bb)
                for c in range(QC):
                    ins = split_product(ACC[:, c * D:(c + 1) * D], lambda a: oT[:, a, c * P:(c + 1) * P],
                                        lambda a: wo_s[:, a, p, :], p == 0 and c == 0, p == PAIRS - 1 and c == QC - 1,
                                        skip_group_check=True)
                ins.then_inc(wout_done, 1)

            def step(b, q):
                s = b * PAIRS + q
                now, prev, last = stage_on(b, q, 0), stage_on(b, q, 1), stage_on(b, q, 2)
                items = step_items(b, q)
                if isinstance(s, int) and s == 0:
                    before = firsts[-2:]
                else:
                    before = [copied(item[2], item[3], s) for item in step_items(b, q - 1)[-2:]]
                lefts = before + [copied(item[2], item[3], s + 1) for item in items]
                for j in range(TPP):
                    if now:
                        scores(b, q, j)
                    if prev:
                        transpose_probs(b, q - 1, j)
                    if last and j == 1:
                        output_projection(b, q - 2)
                    if j == 1 and q % PAIRS == PAIRS - 1 and items:
                        pe.wait_ge(kvT_ready, DC * (items[0][3] + 1))
                    if j % 2 == 1:
                        for n, item in enumerate(items[j // 2:j // 2 + 1]):
                            project(*item, (q + 1) % PAIRS, lefts[j // 2])
                    if prev and j >= 2:
                        v_times_probs(b, q - 1, j - 2)
                for n, item in enumerate(items[2:]):
                    project(*item, 0, lefts[2 + n])

            pe.wait_ge(w_ready, 4)
            steps(pe, step)

            pe.wait_ge(xn_ready, B)

            def gate(i):
                for d in range(DC):
                    ins = T.matmul(SCORE[0][:, i * E:(i + 1) * E], xnT[:, i % 2, d, :], gate_sb[:, d, :],
                                   start=d == 0, stop=d == DC - 1)
                ins.then_inc(gates_done, 1)

            for i in range(TOK):
                wait(pe, xnT_ready, i - 1)
                for d in range(DC):
                    ins = T.transpose(PROJ[i % 2][:, d * P:(d + 1) * P], xn_all[:, i, d * P:(d + 1) * P], ident[:, :])
                ins.then_inc(xnT_done, 1)
                if i >= 1:
                    pe.wait_ge(xnT_ready, i)
                    gate(i - 1)
            pe.wait_ge(xnT_ready, TOK)
            gate(TOK - 1)
            pe.wait_ge(both_ready, 1)
            cols = both[:, :, :].rearrange("p i e -> p (i e)")
            T.matmul(SCORE[1][:, 0:TOK * E], tri[:, :], cols, start=True, stop=False, skip_group_check=True)
            for k in range(1, TOK):
                ins = T.matmul(SCORE[1][:, k * E:TOK * E], ones[:, :], cols[:, 0:(TOK - k) * E], start=False,
                               stop=k == TOK - 1, skip_group_check=True)
            ins.then_inc(ranks_done, 1)
            for i in range(TOK):
                ins = T.matmul(SCORE[1][:, TOK * E:(TOK + 1) * E], ones[:, :], both[:, i, :], start=False,
                               stop=i == TOK - 1, skip_group_check=True)
            ins.then_inc(ranks_done, 1)

            pe.wait_ge(routed, 1)

            def transpose_slots(t, par, u):
                pe.wait_ge(xg_loaded[par], 16 * (u + 1))
                wait(pe, xg_ready, t)
                for d in range(DC):
                    ins = T.transpose(HEADS[:, d * P:(d + 1) * P], xg[:, par, d * P:(d + 1) * P], ident[:, :])
                ins.then_inc(xg_trans, 1)

            def hidden(t, par, w):
                for half in range(2):
                    for m in range(2):
                        if m == 0:
                            wait(pe, silu_done, 2 * (t - 1) + half + 1)
                        else:
                            wait(pe, g_done, 2 * (t - 1) + half + 1)
                        for d in range(DC):
                            at = m * W3AT + d * F + half * FH
                            ins = split_product(banks[2 * half + m][:, :], lambda a: xgT[:, par, a, d, :],
                                                lambda a: W[:, w, a, at:at + FH], d == 0, d == DC - 1)
                        ins.then_inc(h_done, 1)

            def transpose_hidden(t):
                for half in range(2):
                    pe.wait_ge(g_done, 2 * t + half + 1)
                    wait(pe, gT_ready, 2 * (t - 1) + half + 1)
                    for n in range(4):
                        ins = T.transpose(banks[4 + half][:, n * P:(n + 1) * P], g_sb[:, half, n * P:(n + 1) * P],
                                          ident[:, :])
                    ins.then_inc(gT_done, 1)

            def expert_out(t, w):
                pe.wait_ge(gT_ready, 2 * (t + 1))
                wait(pe, y_copied, t)
                for n in range(FC):
                    at = W2AT + n * D
                    ins = split_product(banks[6][:, 0:D], lambda a: gT[:, a, n, :], lambda a: W[:, w, a, at:at + D],
                                        n == 0, n == FC - 1)
                ins.then_inc(y_done, 1)

            transpose_slots(0, 0, 0)

            def tile_step(t, par, u):
                if tile_on(t + 1):
                    transpose_slots(t + 1, 1 - par, u + par)
                if tile_on(t - 1):
                    transpose_hidden(t - 1)
                if tile_on(t):
                    need = pe.value_load(tile_need[0:1, bass.ds(t, 1)], min_val=PIECES, max_val=PIECES * E)
                    w = pe.value_load(tile_parity[0:1, bass.ds(t, 1)], min_val=0, max_val=1)
                    pe.wait_ge(pieces_ready, need)
                    pe.wait_ge(xg_ready, t + 1)
                    hidden(t, par, w)
                if tile_on(t - 1):
                    w = pe.value_load(tile_parity[0:1, bass.ds(t - 1, 1)], min_val=0, max_val=1)
                    expert_out(t - 1, w)

            tile_steps(pe, tile_step)


_INPUTS = ["x", "ctx_1024", "L0_xattn_ln_m_g", "L0_xattn_ln_m_b", "L0_xattn_ln_l_g", "L0_xattn_ln_l_b", "L0_xattn_Wq",
           "L0_xattn_Wkv", "L0_xattn_Wout", "L0_ffn_gate_w", "L0_ffn_w1", "L0_ffn_w3", "L0_ffn_w2"]


def kernel(**inputs):
    import numpy as np
    import concourse.bacc as bacc
    from concourse.bass_utils import run_bass_kernel_spmd

    nc = bacc.Bacc("TRN2", target_bir_lowering=False, num_devices=1)
    arrays, args = {}, []
    for name in _INPUTS:
        a = np.ascontiguousarray(inputs[name])
        arrays[f"in_{name}"] = a
        args.append(nc.dram_tensor(f"in_{name}", a.shape, mybir.dt.from_np(a.dtype), kind="ExternalInput").ap())
    shape = arrays["in_x"].shape
    args.append(nc.dram_tensor("out", shape, mybir.dt.float32, kind="ExternalOutput").ap())
    cross_attention_then_routed_ffn(nc, *args)
    r = run_bass_kernel_spmd(nc, [arrays], core_ids=[0])
    return r.results[0]["out"]
```

```python
import concourse.bass as bass
from concourse import mybir
from contextlib import ExitStack


def cross_attention_then_routed_ffn(
    nc: bass.Bass,
    x: bass.AP,
    context: bass.AP,
    ln_m_g: bass.AP,
    ln_m_b: bass.AP,
    ln_l_g: bass.AP,
    ln_l_b: bass.AP,
    Wq: bass.AP,
    Wkv: bass.AP,
    Wout: bass.AP,
    gate_w: bass.AP,
    w1: bass.AP,
    w3: bass.AP,
    w2: bass.AP,
    out: bass.AP,
):
    fp32, fp32r, bf16 = mybir.dt.float32, mybir.dt.float32r, mybir.dt.bfloat16
    i32, u32 = mybir.dt.int32, mybir.dt.uint32
    ALU = mybir.AluOpType
    ACT = mybir.ActivationFunctionType
    AX = mybir.AxisListType.X

    P = 128
    B, NQ, D = x.shape
    NCTX = context.shape[1]
    NKV = NCTX + NQ
    INNER = Wq.shape[1]
    DH = 64
    PAIRS = INNER // P
    DC = D // P
    QC = NQ // P
    KC = -(-NKV // P)
    KROWS = [min(P, NKV - P * c) for c in range(KC)]
    LNT = 1 + QC
    TPP = 2 * QC
    SCALE = DH ** -0.5
    HALF = INNER // 2
    EPS = 1e-5
    TOK = B * NQ // P
    E, _, F = w1.shape
    FC = F // P
    FH = F // 2
    TILES = (2 * B * NQ + E * P) // P
    REGION = TOK + 1
    SPARE = TILES - 2 * TOK
    TABLE = E * REGION + SPARE
    GROUPS = ((0, TOK // 2), (TOK // 2, TOK - QC), (TOK - QC, TOK))
    assert E == B and TILES % 2 == 0 and QC == 2 and DC == 2 and KC == 3 and PAIRS == 8
    PIECES = 6
    PW = DC * F // 2
    EXPERT_LOADED = 16 * PIECES
    PIECE_STEPS = (3, 5, 6, 7, 8, 9)
    LAST_PIECE_STEPS = (3, 4, 5, 6, 7, 8)
    ROW = D + 2
    W3AT, W2AT, WCOLS = DC * F, 2 * DC * F, 2 * DC * F + FC * D

    sum_dram = nc.dram_tensor("x1_scratch", (TOK * P + P, D), fp32, kind="Internal").ap()
    xs_dram = nc.dram_tensor("slot_rows", (TABLE * P, ROW), fp32, kind="Internal").ap()
    w_dram = nc.dram_tensor("split_weights", (E, 2, P, WCOLS), fp32, kind="Internal").ap()

    stack = ExitStack()
    sems = {}

    def sem(name):
        if name not in sems:
            sems[name] = stack.enter_context(nc.semaphore(name))
        return sems[name]

    with stack:
        def sb(name, shape, dt, ctx=stack):
            return ctx.enter_context(nc.sbuf_tensor(name, shape, dt))

        ident = sb("ident", [P, P], fp32)
        xn_all = sb("xn_all", [P, TOK, ROW], fp32)
        affine = sb("affine", [P, 4, DC], fp32)
        gate_sb = sb("gate_sb", [P, DC, E], fp32)
        gates = sb("gates", [P, TOK, E], fp32)
        w_top = sb("w_top", [P, 2, TOK], fp32)
        slot_of = sb("slot_of", [P, 2, TOK], u32)
        tile_parity = sb("tile_parity", [P, TILES], i32)
        tile_need = sb("tile_need", [P, TILES], i32)
        first_tile = sb("first_tile", [P, E], i32)

        xn_second = sb("xn_second", [P, QC, ROW], fp32)
        filler = sb("filler", [P, ROW], fp32)
        lg = sb("lg", [P, TOK, E], fp32)
        mx = sb("mx", [P, TOK], fp32)
        ex = sb("ex", [P, TOK, E], fp32)
        top = sb("top", [P, TOK, 8], fp32)
        topi = sb("topi", [P, TOK, 8], u32)
        topf = sb("topf", [P, TOK, 8], fp32)
        pick = sb("pick", [P, 2, TOK, E], fp32)
        picked_slot = sb("picked_slot", [P, 2, TOK, E], fp32)
        both = sb("both", [P, TOK, E], bf16)
        tri = sb("tri", [P, P], bf16)
        ones = sb("ones", [P, P], bf16)
        iota_i = sb("iota_i", [P, TILES], i32)
        iota_f = sb("iota_f", [P, TILES], fp32)
        ranks = sb("ranks", [P, TOK, E], fp32)
        count = sb("count", [P, E], fp32)
        region_i = sb("region_i", [P, E], i32)
        region_f = sb("region_f", [P, E], fp32)
        wide = sb("wide", [P, TILES * E], fp32)
        before = sb("before", [P, E + 1, E], fp32)
        tiles_of = sb("tiles_of", [P, E], fp32)
        first_f = sb("first_f", [P, E + 1], fp32)
        slot_f = sb("slot_f", [P, TOK, E], fp32)
        slot_k = sb("slot_k", [P, 2, TOK], fp32)
        need_f = sb("need_f", [P, TILES], fp32)
        tile_row = sb("tile_row", [P, TILES], i32)
        token_i = sb("token_i", [P, TOK + 1], i32)

        attn = ExitStack()
        stage = sb("stage", [P, 4, 2048], fp32, attn)
        raw = stage[:, 0, :].rearrange("p (n w) -> p n w", n=2)
        split = stage[:, 1, :].bitcast(fp32r).rearrange("p (a w) -> p a w", a=2)
        wk_s = sb("wk_s", [P, 2, DC, INNER], fp32r, attn)
        wq_s = sb("wq_s", [P, 2, DC, INNER], fp32r, attn)
        wv_s = sb("wv_s", [P, 2, DC, INNER], fp32r, attn)
        wo_s = sb("wo_s", [P, 2, PAIRS, D], fp32r, attn)
        qT = sb("qT", [P, 2, 2, NQ], fp32r, attn)
        kT = sb("kT", [P, 2, 2, NKV], fp32r, attn)
        probs = sb("probs", [P, TPP, KC * P], fp32, attn)
        probsT = sb("probsT", [P, 2, 2, KC, NQ], fp32r, attn)
        v_s = sb("v_s", [P, 2, KC, INNER], fp32r, attn)
        kvT = sb("kvT", [P, 2, DC, NKV], fp32r, attn)
        xin_flat = sb("xin", [P, LNT * D], fp32, attn)
        xin = xin_flat[:, :].rearrange("p (n d) -> p n d", d=D)
        kvT_f = xin_flat[:, 0:DC * NKV].rearrange("p (c n) -> p c n", c=DC)
        z_flat = sb("z", [P, LNT * D], fp32, attn)
        z = z_flat[:, :].rearrange("p (n d) -> p n d", d=D)
        xnT = [buffer[:, 0:QC * DC * P].rearrange("p (i c n) -> p i c n", i=QC, c=DC)
               for buffer in (xin_flat, z_flat)]
        x1 = sb("x1", [P, QC, D], fp32, attn)
        oT = sb("oT", [P, 2, NQ], fp32r, attn)
        negmax = sb("negmax", [P, 2, TPP], fp32, attn)
        rowsum = sb("rowsum", [P, 2, TPP], fp32, attn)
        rinv = sb("rinv", [P, 2, TPP], fp32, attn)
        stats = sb("stats", [P, 2, LNT, 6], fp32, attn)
        mv = sb("mv", [P, 2, LNT, 2], fp32, attn)
        nve = sb("nve", [P, 2, LNT], fp32, attn)
        nt = sb("nt", [P, 2, LNT], fp32, attn)
        rstd = sb("rstd", [P, 2, LNT], fp32, attn)
        three_halves = sb("three_halves", [P, LNT], fp32, attn)
        attn.close()

        W = sb("W", [P, 2, 2, WCOLS], fp32r)
        xg = sb("xg", [P, 2, ROW], fp32)
        weight = sb("weight", [P, 2, 2], fp32)
        xgT = sb("xgT", [P, 2, 2, DC, P], fp32r)
        act_h = sb("act_h", [P, 2, FH], fp32)
        g_sb = sb("g_sb", [P, 2, FH], fp32)
        gT = sb("gT", [P, 2, FC, P], fp32r)
        y_sb = sb("y_sb", [P, 2, D], fp32)
        y_row = sb("y_row", [P, 2, 1], u32)

        banks = [stack.enter_context(nc.psum_tensor(f"bank{n}", [P, 512], fp32)) for n in range(8)]
        PROJ, SCORE, TRANS, ACC, HEADS = banks[0:2], banks[2:4], banks[4:6], banks[6], banks[7]

        def wait(eng, s, value):
            if not (isinstance(value, int) and value <= 0):
                eng.wait_ge(s, value)

        def split_product(outp, stationary, moving, first, last, **kw):
            for n, (a, b) in enumerate(((0, 0), (0, 1), (1, 0))):
                ins = nc.tensor.matmul(outp, stationary(a), moving(b), start=first and n == 0,
                                       stop=last and n == 2, **kw)
            return ins

        ITEMS = [[(1, "q"), (3, "k")] for _ in range(PAIRS)]
        ITEMS[0] = [(0, ("v", 0, 1)), (1, "q"), (3, "k"), (3, ("v", 0, 2))]
        for c in range(KC):
            ITEMS[1 + c] += [(3, ("v", 1, c))]
        ITEMS[6] += [(3 + d, ("x", 0, d)) for d in range(DC)]
        ITEMS[7] = [(1, "q"), (3, "k"), (3, ("v", 0, 0))]
        OFFSET = [sum(len(i) for i in ITEMS[:q]) for q in range(PAIRS + 1)]
        AHEAD = DC + 3
        assert OFFSET[PAIRS] % 2 == 0

        ROUTING = {3: {0: ("g", 0), 1: ("l", 0), 2: ("g", 1), 3: ("l", 1)},
                   4: {0: ("g", 2), 1: ("l", 2), 2: ("g", 3), 3: ("l", 3)},
                   5: {0: ("g", 4), 1: ("l", 4), 2: ("g", 5), 3: ("l", 5)},
                   6: {0: ("g", 6), 1: ("l", 6), 2: ("r", 0)},
                   8: {1: ("r", 1)}}
        ROUTE_AT = {(5, 0): (0, (0, 1)), (5, 1): (0, (2, 3)), (5, 2): (0, (4, 5)), (5, 3): (0, (6, 7)),
                    (6, 0): (0, (8, 9)), (6, 1): (0, (10, 11)), (6, 2): (0, (12, 13)), (6, 3): (0, (14, 15, 16, 17)),
                    (7, 0): (1, (0, 1)), (7, 1): (1, (2, 3)), (7, 2): (1, (4, 5)), (7, 3): (1, (6, 7)),
                    (8, 0): (1, (8, 9)), (8, 1): (1, (10, 11)), (8, 2): (1, (12, 13, 14)), (8, 3): (1, (15, 16, 17))}

        def final_items(last_q):
            n, found = (B - 1) * OFFSET[PAIRS] + AHEAD + OFFSET[3], [[]] * 5
            for q in range(3, last_q + 1):
                found = [[] for _ in range(5)]
                for at in range(5):
                    own = [what for place, what in (ITEMS[q] if q < PAIRS - 1 else []) if what[0] != "x" and place == at]
                    for what in own + ([ROUTING[q][at]] if at in ROUTING.get(q, {}) else []):
                        found[at].append((n, n % 2, what, B - 1))
                        n += 1
            return found, n

        def step_items(b, q):
            if isinstance(b, int) and b == B - 1 and q >= 3:
                return final_items(q)[0]
            b, q = b + q // PAIRS, q % PAIRS
            found = [[] for _ in range(5)]
            for n, (place, what) in enumerate(ITEMS[q]):
                ahead = what[0] == "x" or what == ("v", 0, 0) or (q == PAIRS - 1 and what in ("q", "k"))
                found[place].append((b * OFFSET[PAIRS] + (AHEAD + OFFSET[q] + n), (AHEAD + OFFSET[q] + n) % 2,
                                           what, b + 1 if ahead else b))
            return found

        NEXT = final_items(8)[1]
        LAST_ROUTING = [(NEXT + n, (NEXT + n) % 2, what, B - 1)
                        for n, what in enumerate([("g", B - 1), ("l", B - 1), ("r", 2)])]

        FIRST_X = [(d, d % 2, ("x", 0, d), 0) for d in range(DC)]
        FIRST_QKV = [(DC + n, (DC + n) % 2, what, 0) for n, what in enumerate(["q", "k", ("v", 0, 0)])]

        head_outputs = [(slice(h * DH, (h + 1) * DH), HEADS[h * DH:(h + 1) * DH, h * NQ:(h + 1) * NQ])
                        for h in range(2)]

        def steps(eng, step):
            for q in range(3):
                step(0, q)
            with eng.Fori(0, B - 1) as b:
                for q in range(3, PAIRS + 3):
                    step(b, q)
            for q in range(3, PAIRS + 3):
                step(B - 1, q)

        def stage_on(b, q, lag):
            return not (isinstance(b, int) and not 0 <= b * PAIRS + q - lag < B * PAIRS)

        def tile_steps(eng, step):
            for t in range(3):
                step(t, t % 2, t // 2)
            with eng.Fori(1, TILES // 2 - 2) as i:
                step(2 * i + 1, 1, i)
                step(2 * i + 2, 0, i + 1)
            for t in range(TILES - 3, TILES + 1):
                step(t, t % 2, t // 2)

        def tile_on(t):
            return not (isinstance(t, int) and not 0 <= t < TILES)

        xin_loaded = sem("xin_loaded")
        xres_loaded, x1_stored = sem("xres_loaded"), sem("x1_stored")
        seeds_ready, newton_step = sem("seeds_ready"), sem("newton_step")
        small_loaded, stage_loaded = sem("small_loaded"), [sem(f"stage_loaded{n}") for n in range(4)]
        w_hi, w_ready, wo_ready = sem("w_hi"), sem("w_ready"), sem("wo_ready")
        consts, turns_taken = sem("consts"), sem("turns_taken")
        newton_last, table_step = sem("newton_last"), sem("table_step")
        prep_step, fin_step, route_step = sem("prep_step"), sem("fin_step"), sem("route_step")
        z_ready, affine_done, kvT_hi, kvT_ready = sem("z_ready"), sem("affine_done"), sem("kvT_hi"), sem("kvT_ready")
        proj_done = sem("proj_done")
        qk_hi, qk_ready, v_hi, v_ready = sem("qk_hi"), sem("qk_ready"), sem("v_hi"), sem("v_ready")
        scores_done, max_done, exp_done = sem("scores_done"), sem("max_done"), sem("exp_done")
        trans_done, pT_hi, pT_ready, av_done = sem("trans_done"), sem("pT_hi"), sem("pT_ready"), sem("av_done")
        rinv_done, probs_ready = sem("rinv_done"), sem("probs_ready")
        oT_hi, oT_ready, wout_done = sem("oT_hi"), sem("oT_ready"), sem("wout_done")
        x1_ready, x1_seeds, xn_ready = sem("x1_ready"), sem("x1_seeds"), sem("xn_ready")
        raw_loaded, hi_split, split_ready = [sem(f"raw_loaded{n}") for n in range(2)], sem("hi_split"), sem("split_ready")
        split_stored, weights_loaded = sem("split_stored"), [sem(f"weights_loaded{n}") for n in range(2)]
        filler_set, xs_filled, scattered = sem("filler_set"), sem("xs_filled"), [sem(f"scattered{n}") for n in range(2)]
        xnT_ready, gates_ready, lg_done = sem("xnT_ready"), sem("gates_ready"), sem("lg_done")
        gate_exp, routed, both_ready, ranks_ready = sem("gate_exp"), sem("routed"), sem("both_ready"), sem("ranks_ready")
        slots_ready = sem("slots_ready")
        xg_loaded, xg_trans, xg_hi, xg_ready = [sem(f"xg_loaded{n}") for n in range(2)], sem("xg_trans"), sem("xg_hi"), sem("xg_ready")
        h_done, silu_done, g_done = sem("h_done"), sem("silu_done"), sem("g_done")
        gT_done, gT_hi, gT_ready = sem("gT_done"), sem("gT_hi"), sem("gT_ready")
        y_done, y_copied, y_added, weight_copied = sem("y_done"), sem("y_copied"), sem("y_added"), sem("weight_copied")
        weight_set, out_stored = sem("weight_set"), sem("out_stored")

        block = stack.enter_context(nc.Block())

        x_rows = x.rearrange("b (c p) d -> b p c d", p=P)
        x1_rows = sum_dram[0:TOK * P, :].rearrange("(b c p) d -> b p c d", p=P, c=QC)
        xs_rows = xs_dram.rearrange("(t p) d -> t p d", p=P)
        out_rows = out.rearrange("b n d -> (b n) d")

        xs_tiles = xs_dram.rearrange("(t p) d -> p t d", p=P)

        def filler_rows(n):
            return filler[:, :].rearrange("p (o d) -> p o d", o=1).broadcast_to([P, n, ROW])

        def stage_of(n, w):
            return stage[:, n, :].rearrange("p (c m) -> p c m", c=w.shape[2])

        def raw_piece(e, n):
            if n < 2 * DC:
                return raw[:, n % 2, :], (w1, w3)[n // DC][e, (n % DC) * P:(n % DC + 1) * P, :]
            return (raw[:, n % 2, :].rearrange("p (c d) -> p c d", d=D),
                    w2[e, (n - 2 * DC) * FH:(n - 2 * DC + 1) * FH, :].rearrange("(c p) d -> p c d", p=P))

        @block.sync
        def _(sp):
            def load_xin(b):
                wait(sp, kvT_ready, DC * b)
                sp.dma_start(xin[0:NCTX, 0, :], context[b]).then_inc(xin_loaded, 16)
                sp.dma_start(xin[:, 1:LNT, :], x_rows[b]).then_inc(xin_loaded, 16)

            def load_xres(b):
                if not (isinstance(b, int) and b == 0):
                    sp.wait_ge(x1_stored, 16 * b)
                    sp.wait_ge(xn_ready, b)
                sp.dma_start(x1[:, :, :], x_rows[b]).then_inc(xres_loaded, 16)

            def store_x1(b):
                sp.wait_ge(x1_ready, 1 + b + 1)
                sp.dma_start(x1_rows[b], x1[:, :, :]).then_inc(x1_stored, 16)

            def load_raw(e, n):
                if not (isinstance(e, int) and e == 0):
                    sp.wait_ge(split_ready, e * PIECES + n - 1)
                else:
                    wait(sp, split_ready, n - 1)
                sp.sem_inc(turns_taken, 1)
                sp.dma_start(*raw_piece(e, n)).then_inc(raw_loaded[n % 2], 16)

            def through_dram(e):
                sp.dma_start(xs_tiles[:, bass.ds(e * REGION, REGION), :], filler_rows(REGION)).then_inc(xs_filled, 16)
                for n in range(PIECES):
                    if n < PIECES - 1:
                        load_raw(e, n + 1)
                    elif not (isinstance(e, int) and e == E - 1):
                        load_raw(e + 1, 0)
                    sp.wait_ge(split_ready, e * PIECES + n + 1)
                    sp.sem_inc(turns_taken, 1)
                    sp.dma_start(w_dram[e].rearrange("a p w -> p a w")[:, :, n * PW:(n + 1) * PW],
                                 split.bitcast(fp32)).then_inc(split_stored, 16)

            def load_expert(e, par):
                for n in range(PIECES):
                    for a in range(2):
                        wait(sp, weights_loaded[a], 16 * (e * PIECES + n))
                        sp.sem_inc(turns_taken, 1)
                        cols = slice(n * PW, (n + 1) * PW)
                        sp.dma_start(W[:, par, a, cols].bitcast(fp32), w_dram[e, a, :, cols]).then_inc(weights_loaded[a], 16)

            sp.wait_ge(consts, 1)
            load_xin(0)
            sp.dma_start(stage[:, 0, :].rearrange("p (c n) -> p c n", c=DC),
                         Wkv[:, 0:INNER].rearrange("(c p) n -> p c n", p=P)).then_inc(stage_loaded[0], 16)
            sp.dma_start(stage[:, 1, :].rearrange("p (c n) -> p c n", c=DC),
                         Wq.rearrange("(c p) n -> p c n", p=P)).then_inc(stage_loaded[1], 16)
            sp.dma_start(stage[:, 2, :].rearrange("p (c n) -> p c n", c=DC),
                         Wkv[:, INNER:2 * INNER].rearrange("(c p) n -> p c n", p=P)).then_inc(stage_loaded[2], 16)
            sp.dma_start(stage[:, 3, :].rearrange("p (c n) -> p c n", c=PAIRS),
                         Wout.rearrange("(c p) n -> p c n", p=P)).then_inc(stage_loaded[3], 16)
            load_xres(0)
            load_xin(1)
            sp.wait_ge(w_ready, 3)
            sp.wait_ge(wo_ready, 1)
            load_raw(0, 0)
            sp.wait_ge(filler_set, 1)
            sp.dma_start(xs_tiles[:, E * REGION:TABLE, :], filler_rows(SPARE)).then_inc(xs_filled, 16)
            sp.dma_start(sum_dram[TOK * P:TOK * P + P, :], filler[:, 0:D]).then_inc(xs_filled, 16)
            with sp.Fori(0, B - 2) as b:
                through_dram(b)
                store_x1(b)
                load_xin(b + 2)
                load_xres(b + 1)
            through_dram(B - 2)
            store_x1(B - 2)
            load_xres(B - 1)
            through_dram(B - 1)
            store_x1(B - 1)

            sp.wait_ge(split_stored, 16 * PIECES * E)
            sp.wait_ge(proj_done, NEXT)
            load_expert(0, 0)
            sp.wait_ge(wout_done, 1 + B * PAIRS)
            load_expert(1, 1)
            sp.wait_ge(routed, 1)
            with sp.Fori(1, E // 2) as i:
                for par in range(2):
                    start = sp.value_load(first_tile[0:1, bass.ds(2 * i + (par - 1), 1)], min_val=1, max_val=TILES)
                    sp.wait_ge(y_done, start)
                    load_expert(2 * i + par, par)

            sp.wait_ge(y_added, 16 * TILES)
            half = TOK * P // 2
            sp.dma_start(out_rows[0:half], sum_dram[0:half, :]).then_inc(out_stored, 16)
            sp.wait_ge(out_stored, 16 * 2)
            sp.wait_ge(x1_stored, 16 * B)

        @block.gpsimd
        def _(pool):
            nc.gpsimd.memset(xin[:, 0, :], 0.0).then_inc(consts, 1)
            nc.gpsimd.memset(ident[:, :], 0.0).then_inc(consts, 1)
            pool.wait_ge(consts, 2)
            nc.gpsimd.affine_select(out=ident[:, :], in_=ident[:, :], compare_op=ALU.not_equal, fill=1.0,
                                    base=0, pattern=[[-1, P]], channel_multiplier=1).then_inc(consts, 1)
            nc.gpsimd.memset(probs[:, :, NKV:KC * P], 0.0).then_inc(consts, 1)

            def split_lo(e, n):
                k = e * PIECES + n
                pool.wait_ge(hi_split, k + 1)
                nc.gpsimd.tensor_tensor(split[:, 1, :], raw[:, n % 2, :], split[:, 0, :],
                                        ALU.subtract).then_inc(split_ready, 1)

            NEWTON = 12
            CHAIN = NEWTON + 1

            def newton(link, k, n):
                y, t = rstd[:, k, 0:n], nt[:, k, 0:n]
                for _ in range(3):
                    link(nc.gpsimd.tensor_tensor(t, y, y, ALU.mult))
                    link(nc.gpsimd.tensor_tensor(t, t, nve[:, k, 0:n], ALU.mult))
                    link(nc.gpsimd.tensor_tensor(t, t, three_halves[:, 0:n], ALU.add))
                    link(nc.gpsimd.tensor_tensor(y, y, t, ALU.mult))

            def pool_chain(start):
                at = [0]

                def link(ins):
                    at[0] += 1
                    ins.then_inc(newton_step, 1)
                    pool.wait_ge(newton_step, start + at[0])
                return link

            def centred(outp, inp, k, n, op):
                by = mv[:, k, 0:n, 0] if op == ALU.subtract else rstd[:, k, 0:n]
                return nc.gpsimd.tensor_tensor(outp, inp, by.unsqueeze(2).broadcast_to([P, n, D]), op)

            def prepare_rstd(b, start):
                pool.wait_ge(seeds_ready, b + 1)
                newton(pool_chain(start), 0, LNT)

            def prepare_z(b, start):
                link = pool_chain(start + NEWTON)
                link(centred(z[:, :, :], xin, 0, LNT, ALU.subtract))
                centred(z[:, :, :], z[:, :, :], 0, LNT, ALU.mult).then_inc(z_ready, 1)

            def finish_batch(b, start):
                link = pool_chain(start)
                pool.wait_ge(x1_seeds, b + 1)
                newton(link, 1, QC)
                rows = xn_all[:, bass.ds(b * QC, QC), 0:D]
                pool.sem_inc(turns_taken, 1)
                link(centred(rows, x1[:, :, :], 1, QC, ALU.subtract))
                pool.sem_inc(turns_taken, 1)
                centred(rows, rows, 1, QC, ALU.mult).then_inc(xn_ready, 1)

            def scatter_part(g, k, half):
                first, end = GROUPS[g]
                middle = (first + end) // 2
                i0, i1 = ((first, middle), (middle, end))[half]
                before = sum(2 * ((b - a) // 2) for a, b in GROUPS[:g])
                if k == 0:
                    pool.wait_ge(slots_ready, g + 1)
                else:
                    pool.wait_ge(scattered[half], 16 * (before + i1 - i0))
                nc.gpsimd.tensor_copy(xn_all[:, i0:i1, D + 1], w_top[:, k, i0:i1]).then_inc(weight_set, 1)
                pool.wait_ge(weight_set, 2 + 4 * g + 2 * k + half + 1)
                for i in range(i0, i1):
                    scatter(xn_all[:, i, :], k, i, scattered[half])

            def scatter_last_group():
                g = len(GROUPS) - 1
                first, end = GROUPS[g]
                pool.wait_ge(slots_ready, g + 1)
                nc.gpsimd.tensor_copy(xn_all[:, first:end, D + 1], w_top[:, 0, first:end]).then_inc(weight_set, 1)
                nc.gpsimd.tensor_copy(xn_second[:, :, D + 1], w_top[:, 1, first:end]).then_inc(weight_set, 1)
                pool.wait_ge(weight_set, 2 + 4 * g + 2)
                for i in range(first, end):
                    scatter(xn_all[:, i, :], 0, i, scattered[0])
                    scatter(xn_second[:, i - first, :], 1, i, scattered[0])

            def scatter(rows, k, i, done):
                nc.gpsimd.indirect_dma_start(
                    out=xs_dram, out_offset=bass.IndirectOffsetOnAxis(ap=slot_of[:, k, i:i + 1], axis=0),
                    in_=rows, in_offset=None).then_inc(done, 16)

            def step(b, q):
                s = b * PAIRS + q
                more = not (isinstance(b, int) and b == B - 1)
                if q == PAIRS - 1 and not more:
                    pool.wait_ge(xs_filled, 16 * (E + 2))
                    scatter_part(0, 0, 0)
                if stage_on(b, q, 0):
                    for j in range(TPP):
                        pool.wait_ge(rinv_done, 2 * s + j // 2 + 1)
                        nc.gpsimd.tensor_tensor(probs[:, j, 0:NKV], probs[:, j, 0:NKV],
                                                rinv[:, q % 2, j:j + 1].broadcast_to([P, NKV]),
                                                ALU.mult).then_inc(probs_ready, 1)
                        if j == 1 and q == PAIRS - 1 and not more:
                            scatter_part(0, 0, 1)
                if q == PAIRS - 1 and not more:
                    scatter_part(0, 1, 0)
                    scatter_part(0, 1, 1)
                if q in PIECE_STEPS and more:
                    split_lo(b, PIECE_STEPS.index(q))
                if q == 4 and more:
                    prepare_rstd(b + 1, CHAIN * (2 * b + 1))
                if q == 5 and more:
                    prepare_z(b + 1, CHAIN * (2 * b + 1))
                if q in LAST_PIECE_STEPS[:-2] and not more:
                    split_lo(b, LAST_PIECE_STEPS.index(q))
                if q == PAIRS + 2 and more:
                    finish_batch(b, CHAIN * (2 * b + 2))
                if q == PAIRS and not more:
                    for k in range(2):
                        for half in range(2):
                            scatter_part(1, k, half)

            nc.gpsimd.memset(three_halves[:, :], 1.5).then_inc(consts, 1)
            nc.gpsimd.memset(filler[:, :], 0.0).then_inc(consts, 1)
            nc.gpsimd.iota(token_i[:, :], pattern=[[P, TOK + 1]], base=0, channel_multiplier=1).then_inc(consts, 1)
            nc.gpsimd.iota(region_i[:, :], pattern=[[REGION * P, E]], base=0, channel_multiplier=0).then_inc(consts, 1)
            nc.gpsimd.iota(iota_i[:, :], pattern=[[1, TILES]], base=0, channel_multiplier=0).then_inc(consts, 1)
            nc.gpsimd.memset(ones[:, :], 1.0).then_inc(consts, 1)
            nc.gpsimd.memset(before[:, :, :], 1.0).then_inc(consts, 1)
            pool.wait_ge(consts, 11)
            nc.gpsimd.tensor_copy(filler[:, D:D + 1], token_i[:, TOK:TOK + 1]).then_inc(filler_set, 1)
            nc.gpsimd.tensor_copy(xn_all[:, :, D], token_i[:, 0:TOK]).then_inc(weight_set, 1)
            nc.gpsimd.tensor_copy(xn_second[:, :, D], token_i[:, TOK - QC:TOK]).then_inc(weight_set, 1)
            nc.gpsimd.affine_select(out=tri[:, :], in_=ones[:, :], compare_op=ALU.is_gt, fill=0.0, base=0,
                                    pattern=[[1, P]], channel_multiplier=-1).then_inc(consts, 1)
            nc.gpsimd.affine_select(out=before[:, :, :], in_=before[:, :, :], compare_op=ALU.is_gt, fill=0.0,
                                    base=0, pattern=[[1, E + 1], [-1, E]], channel_multiplier=0).then_inc(consts, 1)
            prepare_rstd(0, 0)
            prepare_z(0, 0)
            pool.wait_ge(w_hi, 4)
            nc.gpsimd.tensor_tensor(wo_s[:, 1, :, :], stage_of(3, wo_s), wo_s[:, 0, :, :], ALU.subtract).then_inc(wo_ready, 1)
            steps(pool, step)

            scatter_last_group()
            pool.wait_ge(x1_stored, 16 * B)

            def add_rows(t, par):
                pool.wait_ge(y_copied, t + 1)
                wait(pool, y_added, 16 * t)
                if not isinstance(t, int):
                    pool.sem_inc(turns_taken, 1)
                nc.gpsimd.indirect_dma_start(
                    out=sum_dram, out_offset=bass.IndirectOffsetOnAxis(ap=y_row[:, par, :], axis=0),
                    in_=y_sb[:, par, :], in_offset=None, compute_op=ALU.add).then_inc(y_added, 16)

            add_rows(0, 0)
            add_rows(1, 1)
            with pool.Fori(1, TILES // 2) as i:
                add_rows(2 * i, 0)
                add_rows(2 * i + 1, 1)

        @block.scalar
        def _(act):
            def proj_hi(n, bank, what, b, par):
                if what[0] in "glr":
                    return
                if what[0] == "x":
                    act.wait_ge(affine_done, 2 * DC * b + 2 * (what[2] + 1))
                    nc.scalar.activation(kvT[:, 0, what[2], :], kvT_f[:, what[2], :], ACT.Copy).then_inc(kvT_hi, 1)
                    return
                act.wait_ge(proj_done, n + 1)
                if what == "q":
                    nc.scalar.activation(qT[:, par, 0, :], PROJ[bank][:, 0:NQ], ACT.Copy, scale=SCALE).then_inc(qk_hi, 1)
                elif what[0] == "v":
                    half, c = what[1], what[2]
                    nc.scalar.activation(v_s[0:KROWS[c], 0, c, half * HALF:(half + 1) * HALF],
                                         PROJ[bank][0:KROWS[c], :], ACT.Copy).then_inc(v_hi, 1)
                else:
                    nc.scalar.activation(kT[:, par, 0, :], PROJ[bank][:, 0:NKV], ACT.Copy).then_inc(qk_hi, 1)

            for n, vector in enumerate((ln_m_g, ln_m_b, ln_l_g, ln_l_b)):
                act.dma_start(affine[:, n, :], vector.rearrange("(c p) -> p c", p=P), allow_slow_non_contiguous=True).then_inc(small_loaded, 16)
            act.dma_start(gate_sb[:, :, :], gate_w.rearrange("(c p) e -> p c e", p=P)).then_inc(small_loaded, 16)

            def weight_hi(n, w):
                act.wait_ge(stage_loaded[n], 16)
                nc.scalar.activation(w[:, 0, :, :], stage_of(n, w), ACT.Copy).then_inc(w_hi, 1)

            weight_hi(0, wk_s)
            weight_hi(1, wq_s)
            for item in FIRST_X:
                proj_hi(*item, 0)
            weight_hi(2, wv_s)
            weight_hi(3, wo_s)
            for item in FIRST_QKV:
                proj_hi(*item, 0)
            act.wait_ge(consts, 4)

            def piece_hi(e, n):
                act.wait_ge(raw_loaded[n % 2], 16 * (e * (PIECES // 2) + (n // 2 + 1)))
                wait(act, split_stored, 16 * (e * PIECES + n))
                nc.scalar.activation(split[:, 0, :], raw[:, n % 2, :], ACT.Copy).then_inc(hi_split, 1)

            def gates_exp(g):
                tiles = slice(*GROUPS[g])
                act.wait_ge(lg_done, g + 1)
                nc.scalar.activation(ex[:, tiles, :], lg[:, tiles, :], ACT.Exp).then_inc(gate_exp, 1)

            def step(b, q):
                s = b * PAIRS + q
                items = step_items(b, q)
                last_batch = isinstance(b, int) and b == B - 1
                for j in range(TPP):
                    if stage_on(b, q, 1):
                        t, h = (s - 1) * TPP + j, j // 2
                        act.wait_ge(trans_done, t + 1)
                        wait(act, av_done, 2 * (s - 2) + h + 1)
                        nc.scalar.activation(probsT[:, h, 0, :, (j % 2) * P:(j % 2 + 1) * P],
                                             TRANS[j % 2][:, 0:KC * P].rearrange("p (c n) -> p c n", c=KC),
                                             ACT.Copy).then_inc(pT_hi, 1)
                    if stage_on(b, q, 0):
                        t = s * TPP + j
                        act.wait_ge(max_done, t + 1)
                        wait(act, trans_done, t - 3)
                        nc.scalar.activation(probs[:, j, 0:NKV], SCORE[j % 2][:, 0:NKV], ACT.Exp,
                                             bias=negmax[:, q % 2, j:j + 1],
                                             accum_out=rowsum[:, q % 2, j:j + 1]).then_inc(exp_done, 1)
                    if last_batch and q in (5, 7) and j == 0:
                        gates_exp((q - 5) // 2)
                    for item in items[j]:
                        proj_hi(*item, (q + 1) % 2)
                if stage_on(b, q, 1):
                    act.wait_ge(av_done, 2 * s)
                    wait(act, wout_done, 1 + s - 1)
                    for rows, src in head_outputs:
                        nc.scalar.activation(oT[rows, 0, :], src, ACT.Copy).then_inc(oT_hi, 1)
                for item in items[4]:
                    proj_hi(*item, 0)
                pieces = LAST_PIECE_STEPS if last_batch else PIECE_STEPS
                if q in pieces:
                    piece_hi(b, pieces.index(q))

            steps(act, step)

            gates_exp(2)

            def xg_split(t, par):
                act.wait_ge(xg_trans, t + 1)
                wait(act, h_done, 4 * (t - 1))
                nc.scalar.activation(xgT[:, par, 0, :, :], HEADS[:, 0:D].rearrange("p (c n) -> p c n", c=DC),
                                     ACT.Copy).then_inc(xg_hi, 1)

            def load_slots(t, par):
                if tile_on(t):
                    wait(act, xg_trans, t - 1)
                    wait(act, weight_copied, t - 1)
                    row = act.value_load(tile_row[0:1, bass.ds(t, 1)], min_val=0, max_val=TABLE - 1)
                    act.dma_start(xg[:, par, :], xs_rows[row]).then_inc(xg_loaded[par], 16)

            act.wait_ge(scattered[0], 16 * (TOK - QC + 2 * QC))
            act.wait_ge(scattered[1], 16 * (TOK - QC))
            act.wait_ge(routed, 1)
            load_slots(0, 0)
            load_slots(1, 1)
            xg_split(0, 0)

            def tile_step(t, par, u):
                if not (isinstance(t, int) and t + 2 >= TILES):
                    load_slots(t + 2, par)
                if tile_on(t + 1):
                    xg_split(t + 1, 1 - par)
                if tile_on(t - 1):
                    for half in range(2):
                        act.wait_ge(gT_done, 2 * (t - 1) + half + 1)
                        wait(act, y_done, t - 1)
                        nc.scalar.activation(gT[:, 0, 4 * half:4 * half + 4, :],
                                             banks[4 + half][:, :].rearrange("p (c n) -> p c n", c=4),
                                             ACT.Copy).then_inc(gT_hi, 1)
                if tile_on(t):
                    for half in range(2):
                        act.wait_ge(h_done, 4 * t + 2 * half + 1)
                        wait(act, g_done, 2 * (t - 1) + half + 1)
                        nc.scalar.activation(act_h[:, half, :], banks[2 * half][:, :], ACT.Silu).then_inc(silu_done, 1)

            tile_steps(act, tile_step)
            act.wait_ge(y_added, 16 * TILES)
            half = TOK * P // 2
            act.dma_start(out_rows[half:2 * half], sum_dram[half:2 * half, :]).then_inc(out_stored, 16)

        @block.vector
        def _(dve):
            def chain(s, start):
                at = [0]

                def link(ins):
                    at[0] += 1
                    ins.then_inc(s, 1)
                    dve.wait_ge(s, start + at[0])
                return link

            def moments(k, m, tile):
                return nc.vector.bn_stats(stats[:, k, m, :], tile)

            def seed(stage, k, tiles, start, done):
                n = len(tiles)
                bits = nt[:, k, 0:n].bitcast(i32)
                s = (prep_step, fin_step)[k]
                if stage:
                    dve.wait_ge(s, start + stage)
                if stage == 0:
                    for m, tile in enumerate(tiles):
                        ins = moments(k, m, tile)
                elif stage == 1:
                    dve.sem_inc(turns_taken, 1)
                    for m in range(n):
                        ins = nc.vector.bn_aggr(mv[:, k, m, :], stats[:, k, m, :])
                elif stage == 2:
                    once = 1 if k == 0 else n
                    ins = nc.vector.tensor_scalar(nve[:, k, 0:once], mv[:, k, 0:once, 1], EPS, -0.5, ALU.add, ALU.mult)
                    if once < n:
                        ins = nc.vector.tensor_scalar(nve[:, k, once:n], mv[:, k, once:n, 1], -0.5 * (1 + EPS),
                                                      -0.5 * EPS * EPS, ALU.mult, ALU.add)
                elif stage == 3:
                    ins = nc.vector.tensor_scalar(bits, nve[:, k, 0:n].bitcast(i32), 1, None, ALU.logical_shift_right)
                else:
                    ins = nc.vector.tensor_scalar(rstd[:, k, 0:n].bitcast(i32), bits, -1.0, float(0x5F3759DF + 0x3FC00000),
                                                  ALU.mult, ALU.add)
                ins.then_inc(done if stage == 4 else s, 1)

            def prepare_moments(b, m):
                dve.wait_ge(xin_loaded, 32 * (b + 1))
                ins = moments(0, m, xin[:, m, :])
                if m == LNT - 1:
                    ins.then_inc(prep_step, 1)

            def prepare(b, stage):
                if stage == 0:
                    dve.wait_ge(xin_loaded, 32 * (b + 1))
                seed(stage, 0, [xin[:, n, :] for n in range(LNT)], 4 * b, seeds_ready)

            def add_attention(b):
                dve.wait_ge(wout_done, 1 + PAIRS * (b + 1))
                dve.wait_ge(xres_loaded, 16 * (b + 1))
                nc.vector.tensor_tensor(x1[:, :, :], ACC[:, :].rearrange("p (c d) -> p c d", c=QC), x1[:, :, :],
                                        ALU.add).then_inc(x1_ready, 1)

            def finish_batch(b, stage):
                if stage == 0:
                    dve.wait_ge(x1_ready, 1 + b + 1)
                seed(stage, 1, [x1[:, n, :] for n in range(QC)], 4 * b, x1_seeds)

            def evacuate(n, bank, what, b, pair, par):
                src = PROJ[bank]
                if what == "q":
                    dve.wait_ge(qk_hi, 2 * pair + 1)
                    nc.vector.scalar_tensor_tensor(qT[:, par, 1, :], src[:, 0:NQ], SCALE, qT[:, par, 0, :],
                                                   ALU.mult, ALU.subtract).then_inc(qk_ready, 1)
                elif what == "k":
                    dve.wait_ge(qk_hi, 2 * pair + 2)
                    nc.vector.tensor_tensor(kT[:, par, 1, :], src[:, 0:NKV], kT[:, par, 0, :],
                                            ALU.subtract).then_inc(qk_ready, 1)
                elif what[0] == "g":
                    dve.wait_ge(proj_done, n + 1)
                    nc.vector.tensor_copy(xnT[what[1] % 2], src[:, :].rearrange("p (i c n) -> p i c n", i=QC, c=DC)
                                          ).then_inc(xnT_ready, 1)
                elif what[0] == "l":
                    dve.wait_ge(proj_done, n + 1)
                    nc.vector.tensor_copy(gates[:, QC * what[1]:QC * (what[1] + 1), :],
                                          src[:, 0:QC * E].rearrange("p (i e) -> p i e", e=E)).then_inc(gates_ready, 1)
                elif what[0] == "r":
                    dve.wait_ge(proj_done, n + 1)
                    m = GROUPS[what[1]][1] - GROUPS[what[1]][0] + 1
                    nc.vector.tensor_copy(ranks[:, 0:m, :], src[:, 0:m * E].rearrange("p (i e) -> p i e", e=E)
                                          ).then_inc(ranks_ready, 1)
                elif what[0] == "x":
                    d = what[2]
                    dve.wait_ge(proj_done, n + 1)
                    for lo, hi, g in ((0, NCTX, 0), (NCTX, NKV, 2)):
                        nc.vector.tensor_scalar(kvT_f[:, d, lo:hi], src[:, lo:hi], affine[:, g, d:d + 1],
                                                affine[:, g + 1, d:d + 1], ALU.mult, ALU.add).then_inc(affine_done, 1)
                    if d == DC - 1:
                        for m in range(DC):
                            dve.wait_ge(kvT_hi, DC * b + m + 1)
                            nc.vector.tensor_tensor(kvT[:, 1, m, :], kvT_f[:, m, :], kvT[:, 0, m, :],
                                                    ALU.subtract).then_inc(kvT_ready, 1)
                else:
                    half, c = what[1], what[2]
                    dve.wait_ge(v_hi, 2 * KC * b + KC * half + c + 1)
                    cols = slice(half * HALF, (half + 1) * HALF)
                    nc.vector.tensor_tensor(v_s[0:KROWS[c], 1, c, cols], src[0:KROWS[c], :], v_s[0:KROWS[c], 0, c, cols],
                                            ALU.subtract).then_inc(v_ready, 1)

            for stage in range(5):
                prepare(0, stage)
            dve.wait_ge(consts, 13)
            nc.vector.tensor_copy(iota_f[:, :], iota_i[:, :]).then_inc(consts, 1)
            nc.vector.tensor_copy(region_f[:, :], region_i[:, :]).then_inc(consts, 1)
            dve.wait_ge(consts, 15)
            dve.sem_inc(x1_ready, 1)

            def weight_lo(n, w):
                dve.wait_ge(w_hi, n + 1)
                nc.vector.tensor_tensor(w[:, 1, :, :], stage_of(n, w), w[:, 0, :, :], ALU.subtract).then_inc(w_ready, 1)

            weight_lo(0, wk_s)
            weight_lo(1, wq_s)
            dve.wait_ge(small_loaded, 16 * 5)
            for item in FIRST_X:
                evacuate(*item, 0, 0)
            weight_lo(2, wv_s)
            for item in FIRST_QKV:
                evacuate(*item, 0, 0)

            def spread(ap, shape, at):
                return ap.unsqueeze(at).broadcast_to(shape)

            SIGNALS = {1: lg_done, 9: both_ready, 16: slots_ready}
            ROUTE_STAGES = 18
            ROUTE_LINKS = ROUTE_STAGES - len(SIGNALS)

            def route(g, stage):
                v = nc.vector
                first, end = GROUPS[g]
                tiles, n = slice(first, end), end - first
                TE = [P, n, E]
                linked = ROUTE_LINKS * g + len([m for m in range(stage) if m not in SIGNALS])
                if linked:
                    dve.wait_ge(route_step, linked)
                if stage == 0:
                    dve.wait_ge(gates_ready, end // QC)
                    ins = v.tensor_reduce(mx[:, tiles], gates[:, tiles, :], AX, ALU.max)
                elif stage == 1:
                    ins = v.tensor_tensor(lg[:, tiles, :], gates[:, tiles, :], spread(mx[:, tiles], TE, 2), ALU.subtract)
                elif stage == 2:
                    dve.wait_ge(gate_exp, g + 1)
                    ins = v.tensor_reduce(mx[:, tiles], ex[:, tiles, :], AX, ALU.add)
                elif stage == 3:
                    ins = v.reciprocal(mx[:, tiles], mx[:, tiles])
                elif stage == 4:
                    ins = v.tensor_tensor(ex[:, tiles, :], ex[:, tiles, :], spread(mx[:, tiles], TE, 2), ALU.mult)
                elif stage == 5:
                    for i in range(first, end):
                        ins = v.max(top[:, i, :], ex[:, i, :])
                elif stage == 6:
                    for i in range(first, end):
                        ins = v.max_index(topi[:, i, :], top[:, i, :], ex[:, i, :])
                elif stage == 7:
                    ins = v.tensor_copy(topf[:, tiles, 0:2], topi[:, tiles, 0:2])
                elif stage == 8:
                    for k in range(2):
                        ins = v.tensor_tensor(pick[:, k, tiles, :], spread(topf[:, tiles, k], TE, 2),
                                              spread(iota_f[:, 0:E], TE, 1), ALU.is_equal)
                elif stage == 9:
                    ins = v.tensor_tensor(both[:, tiles, :], pick[:, 0, tiles, :], pick[:, 1, tiles, :], ALU.add)
                elif stage == 10:
                    ins = v.tensor_tensor(mx[:, tiles], top[:, tiles, 0], top[:, tiles, 1], ALU.add)
                elif stage == 11:
                    ins = v.reciprocal(mx[:, tiles], mx[:, tiles])
                elif stage == 12:
                    ins = v.tensor_tensor(w_top[:, :, tiles], top[:, tiles, 0:2].rearrange("p i k -> p k i"),
                                          spread(mx[:, tiles], [P, 2, n], 1), ALU.mult)
                elif stage == 13:
                    dve.wait_ge(ranks_ready, g + 1)
                    ins = v.tensor_tensor(slot_f[:, tiles, :], ranks[:, 0:n, :], spread(region_f[:, :], TE, 1), ALU.add)
                elif stage == 14:
                    for k in range(2):
                        ins = v.tensor_tensor(picked_slot[:, k, tiles, :], pick[:, k, tiles, :], slot_f[:, tiles, :], ALU.mult)
                elif stage == 15:
                    ins = v.tensor_reduce(slot_k[:, :, tiles], picked_slot[:, :, tiles, :], AX, ALU.add)
                elif stage == 16:
                    ins = v.tensor_copy(slot_of[:, :, tiles], slot_k[:, :, tiles])
                else:
                    if g == 0:
                        v.tensor_copy(count[:, :], ranks[:, n, :])
                    else:
                        v.tensor_tensor(count[:, :], count[:, :], ranks[:, n, :], ALU.add)
                    ins = v.tensor_tensor(region_f[:, :], region_f[:, :], ranks[:, n, :], ALU.add)
                ins.then_inc(SIGNALS.get(stage, route_step), 1)

            def reciprocal_sums(s, h, par):
                dve.wait_ge(exp_done, TPP * s + 2 * h + 2)
                wait(dve, probs_ready, TPP * (s - 2) + 2 * h + 2)
                nc.vector.reciprocal(rinv[:, par, 2 * h:2 * h + 2], rowsum[:, par, 2 * h:2 * h + 2]).then_inc(rinv_done, 1)

            def step(b, q):
                s = b * PAIRS + q
                items = step_items(b, q)
                more = not (isinstance(b, int) and b == B - 1)
                for j in range(TPP):
                    if stage_on(b, q, 0):
                        dve.wait_ge(scores_done, s * TPP + j + 1)
                        nc.vector.tensor_reduce(negmax[:, q % 2, j:j + 1], SCORE[j % 2][:, 0:NKV], AX, ALU.max,
                                                negate=True).then_inc(max_done, 1)
                    if stage_on(b, q, 1):
                        t, h = (s - 1) * TPP + j, j // 2
                        cols = slice((j % 2) * P, (j % 2 + 1) * P)
                        dve.wait_ge(pT_hi, t + 1)
                        nc.vector.tensor_tensor(probsT[:, h, 1, :, cols],
                                                TRANS[j % 2][:, 0:KC * P].rearrange("p (c n) -> p c n", c=KC),
                                                probsT[:, h, 0, :, cols], ALU.subtract).then_inc(pT_ready, 1)
                    for item in items[j]:
                        evacuate(*item, s + 1, (q + 1) % 2)
                    if j == 2 and stage_on(b, q, 0):
                        reciprocal_sums(s, 0, q % 2)
                    if j == 2 and q == PAIRS + 1:
                        add_attention(b)
                    if q == 3 and more and j < LNT:
                        prepare_moments(b + 1, j)
                    if q == 4 and more:
                        prepare(b + 1, 1 + j)
                    if q == PAIRS + 2:
                        finish_batch(b, j)
                        if j == TPP - 1:
                            finish_batch(b, TPP)
                    if (q, j) in ROUTE_AT and not more:
                        for stage in ROUTE_AT[q, j][1]:
                            route(ROUTE_AT[q, j][0], stage)
                if stage_on(b, q, 0):
                    reciprocal_sums(s, 1, q % 2)
                if stage_on(b, q, 1):
                    dve.wait_ge(oT_hi, 2 * s)
                    for rows, src in head_outputs:
                        nc.vector.tensor_tensor(oT[rows, 1, :], src, oT[rows, 0, :], ALU.subtract).then_inc(oT_ready, 1)
                for item in items[4]:
                    evacuate(*item, 0, 0)
                if q in LAST_PIECE_STEPS[-2:] and not more:
                    n = LAST_PIECE_STEPS.index(q)
                    dve.wait_ge(hi_split, b * PIECES + n + 1)
                    nc.vector.tensor_tensor(split[:, 1, :], raw[:, n % 2, :], split[:, 0, :],
                                            ALU.subtract).then_inc(split_ready, 1)

            def finish_last_batch():
                dve.wait_ge(x1_seeds, B)
                link = chain(newton_last, 0)
                y, t = rstd[:, 1, 0:QC], nt[:, 1, 0:QC]
                for _ in range(3):
                    link(nc.vector.tensor_tensor(t, y, y, ALU.mult))
                    link(nc.vector.tensor_tensor(t, t, nve[:, 1, 0:QC], ALU.mult))
                    link(nc.vector.scalar_tensor_tensor(y, t, 1.5, y, ALU.add, ALU.mult))
                for rows in (xn_all[:, TOK - QC:TOK, :], xn_second[:, :, :]):
                    for m in range(QC):
                        ins = nc.vector.tensor_scalar(rows[:, m, 0:D], x1[:, m, :], mv[:, 1, m, 0:1],
                                                      rstd[:, 1, m:m + 1], ALU.subtract, ALU.mult)
                    ins.then_inc(xn_ready, 1)

            steps(dve, step)

            finish_last_batch()

            for item in LAST_ROUTING[0:2]:
                evacuate(*item, 0, 0)
            for stage in range(10):
                route(2, stage)
            evacuate(*LAST_ROUTING[2], 0, 0)
            for stage in range(10, ROUTE_STAGES):
                route(2, stage)

            link = chain(table_step, 0)

            def wide_as(shape):
                names = "abc"[:len(shape) - 1]
                n = shape[1] * shape[2]
                return wide[:, 0:n].rearrange(f"p ({' '.join(names)}) -> p {' '.join(names)}",
                                              **dict(zip(names, shape[1:])))

            v = nc.vector
            steps_of = TOK - 1
            dve.wait_ge(route_step, len(GROUPS) * ROUTE_LINKS)
            link(v.tensor_scalar(need_f[:, 0:steps_of], iota_f[:, 1:TOK], float(P), None, ALU.mult))
            shape = [P, E, steps_of]
            link(v.tensor_tensor(wide_as(shape), spread(count[:, :], shape, 2),
                                 spread(need_f[:, 0:steps_of], shape, 1), ALU.is_gt))
            link(v.tensor_reduce(tiles_of[:, :], wide_as(shape), AX, ALU.add))
            link(v.tensor_scalar(tiles_of[:, :], tiles_of[:, :], 1.0, None, ALU.add))
            shape = [P, E + 1, E]
            link(v.tensor_tensor(wide_as(shape), before[:, :, :], spread(tiles_of[:, :], shape, 1), ALU.mult))
            link(v.tensor_reduce(first_f[:, :], wide_as(shape), AX, ALU.add))
            link(v.tensor_copy(first_tile[:, :], first_f[:, 0:E]))
            shape = [P, TILES, E]
            begun = wide_as(shape)
            link(v.tensor_tensor(begun, spread(iota_f[:, :], shape, 2), spread(first_f[:, 1:E + 1], shape, 1), ALU.is_ge))
            link(v.tensor_reduce(need_f[:, :], begun[:, :, 0:E - 1], AX, ALU.add))
            link(v.tensor_copy(tile_need[:, :], need_f[:, :]))
            link(v.tensor_scalar(tile_parity[:, :], tile_need[:, :], 1, None, ALU.bitwise_and))
            link(v.tensor_scalar(need_f[:, :], need_f[:, :], float(EXPERT_LOADED), float(EXPERT_LOADED), ALU.mult, ALU.add))
            link(v.tensor_copy(tile_need[:, :], need_f[:, :]))
            link(v.tensor_scalar(tiles_of[:, :], tiles_of[:, :], -1.0, float(REGION), ALU.mult, ALU.add))
            link(v.tensor_tensor(begun, begun, spread(tiles_of[:, :], shape, 1), ALU.mult))
            link(v.tensor_reduce(need_f[:, :], begun, AX, ALU.add))
            link(v.tensor_tensor(need_f[:, :], need_f[:, :], iota_f[:, :], ALU.add))
            v.tensor_copy(tile_row[:, :], need_f[:, :]).then_inc(routed, 1)
            dve.wait_ge(routed, 1)
            dve.wait_ge(xn_ready, B + 1)

            def xg_split(t, par):
                dve.wait_ge(xg_hi, t + 1)
                nc.vector.tensor_tensor(xgT[:, par, 1, :, :], HEADS[:, 0:D].rearrange("p (c n) -> p c n", c=DC),
                                        xgT[:, par, 0, :, :], ALU.subtract).then_inc(xg_ready, 1)

            def copy_weight(t, par):
                wait(dve, y_copied, t - 1)
                nc.vector.tensor_copy(weight[:, par, :], xg[:, par, D:ROW]).then_inc(weight_copied, 1)

            xg_split(0, 0)
            copy_weight(0, 0)

            def tile_step(t, par, u):
                if tile_on(t + 1):
                    xg_split(t + 1, 1 - par)
                if tile_on(t - 1):
                    for half in range(2):
                        dve.wait_ge(gT_hi, 2 * (t - 1) + half + 1)
                        chunk = slice(4 * half, 4 * half + 4)
                        nc.vector.tensor_tensor(gT[:, 1, chunk, :], banks[4 + half][:, :].rearrange("p (c n) -> p c n", c=4),
                                                gT[:, 0, chunk, :], ALU.subtract).then_inc(gT_ready, 1)
                if tile_on(t):
                    for half in range(2):
                        dve.wait_ge(h_done, 4 * t + 2 * half + 2)
                        dve.wait_ge(silu_done, 2 * t + half + 1)
                        wait(dve, gT_done, 2 * (t - 1) + half + 1)
                        nc.vector.tensor_tensor(g_sb[:, half, :], banks[2 * half + 1][:, :], act_h[:, half, :],
                                                ALU.mult).then_inc(g_done, 1)
                if tile_on(t - 1):
                    dve.wait_ge(y_done, t)
                    wait(dve, y_added, 16 * (t - 2))
                    nc.vector.tensor_copy(y_row[:, 1 - par, :], weight[:, 1 - par, 0:1])
                    nc.vector.tensor_scalar(y_sb[:, 1 - par, :], banks[6][:, 0:D], weight[:, 1 - par, 1:2], None,
                                            ALU.mult).then_inc(y_copied, 1)
                if tile_on(t + 1):
                    copy_weight(t + 1, 1 - par)

            tile_steps(dve, tile_step)

        @block.tensor
        def _(pe):
            T = nc.tensor

            def copied(what, b, pair):
                if what in ("q", "k"):
                    return qk_ready, 2 * pair + 1 + (what == "k")
                if what[0] == "x":
                    return kvT_ready, DC * b + what[2] + 1
                if what[0] in "glr":
                    return {"g": xnT_ready, "l": gates_ready, "r": ranks_ready}[what[0]], what[1] + 1
                return v_ready, 2 * KC * b + KC * what[1] + what[2] + 1

            def project(n, bank, what, b, pair_in_batch, left):
                if left:
                    pe.wait_ge(*left)
                if what in ("q", "k"):
                    w, lo = (wq_s, NCTX) if what == "q" else (wk_s, 0)
                    cols = slice(pair_in_batch * P, (pair_in_batch + 1) * P)
                    for d in range(DC):
                        ins = split_product(PROJ[bank][:, 0:NKV - lo], lambda a: w[:, a, d, cols],
                                            lambda a: kvT[:, a, d, lo:NKV], d == 0, d == DC - 1)
                elif what[0] == "x":
                    d = what[2]
                    pe.wait_ge(z_ready, b + 1)
                    for n_tile in range(LNT):
                        rows = NCTX if n_tile == 0 else P
                        at = 0 if n_tile == 0 else NCTX + (n_tile - 1) * P
                        ins = T.transpose(PROJ[bank][:, at:at + rows], z[0:rows, n_tile, d * P:(d + 1) * P],
                                          ident[0:rows, 0:rows])
                elif what[0] == "g":
                    pe.wait_ge(xn_ready, what[1] + 1)
                    for i in range(QC):
                        for d in range(DC):
                            at = (i * DC + d) * P
                            ins = T.transpose(PROJ[bank][:, at:at + P],
                                              xn_all[:, QC * what[1] + i, d * P:(d + 1) * P], ident[:, :])
                elif what[0] == "l":
                    pe.wait_ge(xnT_ready, what[1] + 1)
                    for i in range(QC):
                        for d in range(DC):
                            ins = T.matmul(PROJ[bank][:, i * E:(i + 1) * E], xnT[what[1] % 2][:, i, d, :],
                                           gate_sb[:, d, :], start=d == 0, stop=d == DC - 1)
                elif what[0] == "r":
                    pe.wait_ge(both_ready, what[1] + 1)
                    first, end = GROUPS[what[1]]
                    m = end - first
                    cols = both[:, :, :].rearrange("p i e -> p (i e)")[:, first * E:end * E]
                    T.matmul(PROJ[bank][:, 0:m * E], tri[:, :], cols, start=True, stop=False, skip_group_check=True)
                    for k in range(1, m):
                        T.matmul(PROJ[bank][:, k * E:m * E], ones[:, :], cols[:, 0:(m - k) * E], start=False,
                                 stop=False, skip_group_check=True)
                    for i in range(m):
                        ins = T.matmul(PROJ[bank][:, m * E:(m + 1) * E], ones[:, :], cols[:, i * E:(i + 1) * E],
                                       start=False, stop=i == m - 1, skip_group_check=True)
                else:
                    half, c = what[1], what[2]
                    rows = slice(c * P, c * P + KROWS[c])
                    for d in range(DC):
                        ins = split_product(PROJ[bank][0:KROWS[c], :], lambda a: kvT[:, a, d, rows],
                                            lambda a: wv_s[:, a, d, half * HALF:(half + 1) * HALF],
                                            d == 0, d == DC - 1)
                ins.then_inc(proj_done, 1)

            pe.sem_inc(wout_done, 1)
            pe.wait_ge(consts, 3)
            firsts = [copied(item[2], 0, 0) for item in FIRST_X + FIRST_QKV]
            for item in FIRST_X:
                project(*item, 0, None)
            pe.wait_ge(kvT_ready, DC)
            for n, item in enumerate(FIRST_QKV):
                pe.wait_ge(w_ready, {"q": 2, "k": 2}.get(item[2], 3))
                project(*item, 0, firsts[n])

            def scores(b, q, j):
                s = b * PAIRS + q
                t = s * TPP + j
                h, c, par = j // 2, j % 2, q % 2
                if j == 0:
                    pe.wait_ge(qk_ready, 2 * (s + 1))
                wait(pe, exp_done, t - 1)
                rows = slice(h * DH, (h + 1) * DH)
                split_product(SCORE[j % 2][:, 0:NKV], lambda a: qT[rows, par, a, c * P:(c + 1) * P],
                              lambda a: kT[rows, par, a, :], True, True).then_inc(scores_done, 1)

            def transpose_probs(b, q, j):
                s = b * PAIRS + q
                pe.wait_ge(probs_ready, s * TPP + j + 1)
                wait(pe, pT_ready, s * TPP + j - 1)
                for c in range(KC):
                    ins = T.transpose(TRANS[j % 2][:, c * P:(c + 1) * P], probs[:, j, c * P:(c + 1) * P],
                                      ident[:, :])
                ins.then_inc(trans_done, 1)

            def v_times_probs(b, q, h):
                s = b * PAIRS + q
                bb, p = b + q // PAIRS, q % PAIRS
                if h == 0:
                    wait(pe, oT_ready, 2 * s)
                    pe.wait_ge(v_ready, 2 * KC * bb + (KC if p < PAIRS // 2 else 2 * KC))
                pe.wait_ge(pT_ready, s * TPP + 2 * h + 2)
                cols = slice(p * P, (p + 1) * P)
                for c in range(KC):
                    ins = split_product(HEADS[:, h * NQ:(h + 1) * NQ], lambda a: v_s[0:KROWS[c], a, c, cols],
                                        lambda a: probsT[0:KROWS[c], h, a, c, :], c == 0, c == KC - 1)
                ins.then_inc(av_done, 1)

            def output_projection(b, q):
                s = b * PAIRS + q
                bb, p = b + q // PAIRS, q % PAIRS
                pe.wait_ge(oT_ready, 2 * s + 2)
                if isinstance(s, int) and s == 0:
                    pe.wait_ge(wo_ready, 1)
                if p == 0:
                    pe.wait_ge(x1_ready, 1 + bb)
                for c in range(QC):
                    ins = split_product(ACC[:, c * D:(c + 1) * D], lambda a: oT[:, a, c * P:(c + 1) * P],
                                        lambda a: wo_s[:, a, p, :], p == 0 and c == 0, p == PAIRS - 1 and c == QC - 1,
                                        skip_group_check=True)
                ins.then_inc(wout_done, 1)

            def final_items_and_pairs(last_q):
                return [(item, (B - 1) * PAIRS + q + 1) for q in range(3, last_q + 1) for item in sum(final_items(q)[0], [])]

            def step(b, q):
                s = b * PAIRS + q
                now, prev, last = stage_on(b, q, 0), stage_on(b, q, 1), stage_on(b, q, 2)
                items = step_items(b, q)
                if isinstance(s, int) and s == 0:
                    before = firsts[-2:]
                else:
                    earlier = [(item, s) for item in sum(step_items(b, q - 1), [])]
                    if isinstance(b, int) and b == B - 1 and q > 3:
                        earlier = final_items_and_pairs(q - 1)
                    before = [copied(item[2], item[3], pair) for item, pair in earlier[-2:]]
                lefts = before + [copied(item[2], item[3], s + 1) for item in sum(items, [])]
                for j in range(TPP):
                    if now:
                        scores(b, q, j)
                    if prev:
                        transpose_probs(b, q - 1, j)
                    if last and j == 1:
                        output_projection(b, q - 2)
                    if j == 1 and q % PAIRS == PAIRS - 1 and items[j]:
                        pe.wait_ge(kvT_ready, DC * (items[j][0][3] + 1))
                    for item in items[j]:
                        project(*item, (q + 1) % PAIRS, lefts.pop(0))
                    late = q % PAIRS in (4, 5)
                    if prev and j == (3 if late else 2):
                        v_times_probs(b, q - 1, 0)
                    if prev and j == 3:
                        v_times_probs(b, q - 1, 1)
                for item in items[4]:
                    project(*item, 0, lefts.pop(0))

            steps(pe, step)

            earlier = final_items_and_pairs(PAIRS)[-2:] + [(LAST_ROUTING[0], 0)]
            left = [copied(item[2], item[3], pair) for item, pair in earlier]
            for item, wait_for in zip(LAST_ROUTING, left):
                project(*item, 0, wait_for)

            pe.wait_ge(routed, 1)

            def transpose_slots(t, par, u):
                pe.wait_ge(xg_loaded[par], 16 * (u + 1))
                wait(pe, xg_ready, t)
                for d in range(DC):
                    ins = T.transpose(HEADS[:, d * P:(d + 1) * P], xg[:, par, d * P:(d + 1) * P], ident[:, :])
                ins.then_inc(xg_trans, 1)

            def hidden(t, par, w):
                for half in range(2):
                    for m in range(2):
                        if m == 0:
                            wait(pe, silu_done, 2 * (t - 1) + half + 1)
                        else:
                            wait(pe, g_done, 2 * (t - 1) + half + 1)
                        for d in range(DC):
                            at = m * W3AT + d * F + half * FH
                            ins = split_product(banks[2 * half + m][:, :], lambda a: xgT[:, par, a, d, :],
                                                lambda a: W[:, w, a, at:at + FH], d == 0, d == DC - 1)
                        ins.then_inc(h_done, 1)

            def transpose_hidden(t):
                for half in range(2):
                    pe.wait_ge(g_done, 2 * t + half + 1)
                    wait(pe, gT_ready, 2 * (t - 1) + half + 1)
                    for n in range(4):
                        ins = T.transpose(banks[4 + half][:, n * P:(n + 1) * P], g_sb[:, half, n * P:(n + 1) * P],
                                          ident[:, :])
                    ins.then_inc(gT_done, 1)

            def expert_out(t, w):
                pe.wait_ge(gT_ready, 2 * (t + 1))
                wait(pe, y_copied, t)
                for n in range(FC):
                    at = W2AT + n * D
                    ins = split_product(banks[6][:, 0:D], lambda a: gT[:, a, n, :], lambda a: W[:, w, a, at:at + D],
                                        n == 0, n == FC - 1)
                ins.then_inc(y_done, 1)

            transpose_slots(0, 0, 0)

            def tile_step(t, par, u):
                if tile_on(t + 1):
                    transpose_slots(t + 1, 1 - par, u + par)
                if tile_on(t - 1):
                    transpose_hidden(t - 1)
                if tile_on(t):
                    need = pe.value_load(tile_need[0:1, bass.ds(t, 1)], min_val=EXPERT_LOADED, max_val=EXPERT_LOADED * E)
                    w = pe.value_load(tile_parity[0:1, bass.ds(t, 1)], min_val=0, max_val=1)
                    for loaded in weights_loaded:
                        pe.wait_ge(loaded, need)
                    pe.wait_ge(xg_ready, t + 1)
                    hidden(t, par, w)
                if tile_on(t - 1):
                    w = pe.value_load(tile_parity[0:1, bass.ds(t - 1, 1)], min_val=0, max_val=1)
                    expert_out(t - 1, w)

            tile_steps(pe, tile_step)


_INPUTS = ["x", "ctx_1024", "L0_xattn_ln_m_g", "L0_xattn_ln_m_b", "L0_xattn_ln_l_g", "L0_xattn_ln_l_b", "L0_xattn_Wq",
           "L0_xattn_Wkv", "L0_xattn_Wout", "L0_ffn_gate_w", "L0_ffn_w1", "L0_ffn_w3", "L0_ffn_w2"]


def kernel(**inputs):
    import numpy as np
    import concourse.bacc as bacc
    from concourse.bass_utils import run_bass_kernel_spmd

    nc = bacc.Bacc("TRN2", target_bir_lowering=False, num_devices=1)
    arrays, args = {}, []
    for name in _INPUTS:
        a = np.ascontiguousarray(inputs[name])
        arrays[f"in_{name}"] = a
        args.append(nc.dram_tensor(f"in_{name}", a.shape, mybir.dt.from_np(a.dtype), kind="ExternalInput").ap())
    shape = arrays["in_x"].shape
    args.append(nc.dram_tensor("out", shape, mybir.dt.float32, kind="ExternalOutput").ap())
    cross_attention_then_routed_ffn(nc, *args)
    r = run_bass_kernel_spmd(nc, [arrays], core_ids=[0])
    return r.results[0]["out"]
```
